# Optimizing a Trainium2 kernel written in Bass

```python
import numpy as np
import jax
import jax.numpy as jnp

def _softmax(x, axis=-1):
    return jax.nn.softmax(x, axis=axis)

def _gelu(x):
    return jax.nn.gelu(x, approximate=True)

def _silu(x):
    return jax.nn.silu(x)

def _sigmoid(x):
    return jax.nn.sigmoid(x)

def _layernorm(x, axis=-1, eps=1e-05):
    m = jnp.mean(x, axis=axis, keepdims=True)
    v = jnp.var(x, axis=axis, keepdims=True)
    return (x - m) / jnp.sqrt(v + eps)

def _scatter_add(tgt, idx, src, axis=0):
    return tgt.at[idx].add(src)

def _segment_sum(src, seg, n):
    return jax.ops.segment_sum(src, seg, n)
kernel_name = 'mk_adj_resnorm_d1_adj_r2_b3974e'

def setup_inputs(seed: int=0):
    np.random.seed(seed)
    _w = jnp.asarray

    def _rec_inputs():
        import jax
        import jax.numpy as jnp
        _gk = jax.random.key(seed)
        x = -0.0002928 + 1 * jax.random.normal(jax.random.fold_in(_gk, 1), (2048, 512), jnp.float32)
        _w = (1.0 + jnp.arange(2048, dtype=jnp.float32)) ** (-0.5)
        _w = _w / _w.mean()
        _pij = jnp.clip(0.00195312 * _w[:, None] * _w[None, :], 0.0, 1.0)
        _a = jax.random.uniform(jax.random.fold_in(_gk, 2), (2048, 2048)) < _pij
        _af = _a.astype(jnp.float32)
        adj = _af
        return (x, adj)
    x, adj = _rec_inputs()

    def _L0_gnn_setup():
        import jax, jax.numpy as jnp
        import numpy as np
        N = 2048
        D_IN = 512
        H = 16
        DH = D_IN // H
        ALPHA = 0.2
        MASK_VAL = -65500.0
        key = jax.random.key(seed)
        ks = jax.random.split(key, 7)
        x = jax.random.normal(ks[0], (N, D_IN), dtype=jnp.float32)
        adj = jax.random.randint(ks[1], (N, N), 0, 2).astype(jnp.float32)
        s = 1.0 / np.sqrt(D_IN)
        W_seq = jax.random.normal(ks[2], (D_IN, D_IN), dtype=jnp.float32) * s
        a1 = jax.random.normal(ks[3], (DH,), dtype=jnp.float32) / np.sqrt(DH)
        a2 = jax.random.normal(ks[4], (DH,), dtype=jnp.float32) / np.sqrt(DH)
        W_out = jax.random.normal(ks[5], (D_IN, D_IN), dtype=jnp.float32) * s
        b_out = jax.random.normal(ks[6], (D_IN,), dtype=jnp.float32) * 0.01
        return {'x': x, 'adj': adj, 'W_seq': W_seq, 'a1': a1, 'a2': a2, 'W_out': W_out, 'b_out': b_out}
    _L0_gnn_all = _L0_gnn_setup()
    _L0_gnn_in = {k: v for k, v in _L0_gnn_all.items() if k in ('W_seq', 'a1', 'a2', 'W_out', 'b_out')}
    del _L0_gnn_all
    return {'x': x, 'adj': adj, 'L0_gnn_W_seq': _L0_gnn_in['W_seq'], 'L0_gnn_a1': _L0_gnn_in['a1'], 'L0_gnn_a2': _L0_gnn_in['a2'], 'L0_gnn_W_out': _L0_gnn_in['W_out'], 'L0_gnn_b_out': _L0_gnn_in['b_out']}

def reference(x, adj, L0_gnn_W_seq, L0_gnn_a1, L0_gnn_a2, L0_gnn_W_out, L0_gnn_b_out):
    import jax
    import jax.numpy as jnp

    def _L0_gnn_ref(x, adj, W_seq, a1, a2, W_out, b_out):
        import jax, jax.numpy as jnp
        import numpy as np
        N = 2048
        D_IN = 512
        H = 16
        DH = D_IN // H
        ALPHA = 0.2
        MASK_VAL = -65500.0
        seq = (x @ W_seq).reshape(N, H, DH)
        score1 = jnp.einsum('nhd,d->hn', seq, a1)
        score2 = jnp.einsum('nhd,d->hn', seq, a2)
        scores = score1[:, :, None] + score2[:, None, :]
        scores = jax.nn.leaky_relu(scores, negative_slope=ALPHA)
        scores = scores + (1.0 - adj)[None, :, :] * MASK_VAL
        attn = jax.nn.softmax(scores, axis=-1)
        hidden = jnp.einsum('hij,jhd->ihd', attn, seq).reshape(N, D_IN)
        hidden = hidden @ W_out + b_out
        return jax.nn.elu(hidden)
    x = _layernorm(x + _L0_gnn_ref(x, adj, L0_gnn_W_seq, L0_gnn_a1, L0_gnn_a2, L0_gnn_W_out, L0_gnn_b_out), axis=-1)
    return x

_drawn_inputs = setup_inputs


def setup_inputs(seed=0):
    import zlib

    import numpy as np

    out = dict(_drawn_inputs(seed))
    spreads = {}
    factors = {'L0_gnn_b_out': 7.183}
    for name, (base, spread) in spreads.items():
        noise = np.random.default_rng([zlib.crc32(name.encode()), seed]).standard_normal(out[name].shape)
        drawn = base * np.exp(spread * noise) if base else spread * noise
        out[name] = jnp.asarray(drawn.astype(out[name].dtype))
    for name, factor in factors.items():
        out[name] = (out[name] * factor).astype(out[name].dtype)
    return out
```

```python
from contextlib import ExitStack

import concourse.bass as bass
from concourse import mybir

F32 = mybir.dt.float32
F16 = mybir.dt.float16
BF16 = mybir.dt.bfloat16
U32 = mybir.dt.uint32
ALU = mybir.AluOpType
ACT = mybir.ActivationFunctionType
AX = mybir.AxisListType

P = 128
N, D, H, DH = 2048, 512, 16, 32
NT = N // P
KT = D // P
SLOPE = 0.2
EPS = 1e-5

VW = 2 * DH + 2
COL_B, COL_B1, COL_A1 = DH, 2 * DH, 2 * DH + 1
HW = DH + 1
LO = 2.0 ** 11
TOP = 2.0 ** 13
SIGN_SCALE = 2.0 ** 60
TINY = 2.0 ** -100

RING = 4
GRP = 4
GROUPS = H // GRP
ITB = 3
BANKS = -(-NT // ITB)
STEPS = NT // RING
ACT_PER_HEAD = NT - STEPS


def gat_kernel(nc, x, adj, W_seq, a1, a2, W_out, b_out, out):
    with ExitStack() as ctx:
        def sb(name, shape, dt):
            return ctx.enter_context(nc.sbuf_tensor(name, shape, dt))

        def sem(name):
            return ctx.enter_context(nc.semaphore(name))

        adjT = sb("adjT", [P, NT, N], BF16)
        Vp = sb("Vp", [P, NT, H, 2, VW], F16)
        acc = sb("acc", [P, NT, H * HW], F32)
        abc = sb("abc", [P, 2, N], F32)
        tring = sb("tring", [P, RING, N], BF16)
        adjb = sb("adjb", [P, 2, N], BF16)
        ab = sb("ab", [P, NT, 2 * H], F32)
        nbs = sb("nbs", [P, NT, H], F32)
        idf = sb("idf", [P, P], F32)
        idb = sb("idb", [P, P], BF16)
        Mb = sb("Mb", [P, 2 * H], F32)
        vsc = sb("vsc", [P, H], F32)
        vinv = sb("vinv", [P, H], F32)
        deg = sb("deg", [P, 2], F32)
        noedge = sb("noedge", [P, 2], F32)

        seq = acc[:, :, 0:D]
        W_sb = abc[:, 0, :].rearrange("p (k n) -> p k n", k=KT)
        xs = abc[:, 1, 0:2 * D].rearrange("p (r n) -> p r n", r=2)
        xT = abc[:, 1, 2 * D:4 * D].rearrange("p (r n) -> p r n", r=2)
        aT = abc[0:H, 0, :]
        E = abc[:, 1, 0:2 * NT * H].rearrange("p (t s h) -> p t s h", t=NT, s=2)
        XW = NT * DH
        xp = [abc[:, 1, (1 + r) * XW:(2 + r) * XW].rearrange("p (t d) -> p t d", t=NT) for r in range(2)]
        mx = abc[:, 1, 3 * XW:3 * XW + 32]
        diag = abc[:, 1, 3 * XW + 32:3 * XW + 64]
        ones = abc[:, 1, 3 * XW + 64:3 * XW + 64 + P]
        mcol = abc[:, 1, 3 * XW + 200:3 * XW + 201]
        stage = tring[:].rearrange("p r n -> p (r n)").bitcast(F32).rearrange("p (r n) -> p r n", r=2)
        wa = acc[:, 0:2 * KT, D:D + H].rearrange("p (k s) h -> p k s h", s=2)
        work = adjb[:].rearrange("p r n -> p (r n)").bitcast(F32)
        comb = work[:, 0:NT * VW].rearrange("p (t c) -> p t c", t=NT)
        o = NT * VW
        hlo = work[:, o:o + 2 * ITB * VW].rearrange("p (r t c) -> p r t c", r=2, t=ITB)
        o += 2 * ITB * VW
        glo = work[:, o:o + 2 * GRP * HW].rearrange("p (r g c) -> p r g c", r=2, g=GRP)
        o += 2 * GRP * HW
        gsum = work[:, o:o + 2 * GRP * HW].rearrange("p (r g c) -> p r g c", r=2, g=GRP)

        Wo_sb = abc[:, 0, :].rearrange("p (k n) -> p k n", k=KT)
        free = Vp[:].rearrange("p t h s c -> p (t h s c)").bitcast(F32)

        def ring(k):
            return free[:, 2 * k * D:2 * (k + 1) * D].rearrange("p (r n) -> p r n", r=2)
        xr, hid, hT, zt, et, yt, ot = (ring(k) for k in range(7))
        bout = free[:, 14 * D:15 * D]
        rden = free[:, 15 * D:15 * D + NT * H].rearrange("p (t h) -> p t h", t=NT)
        stats = free[:, 16 * D:16 * D + 12].rearrange("p (r c) -> p r c", r=2)
        mv = free[:, 16 * D + 12:16 * D + 16].rearrange("p (r c) -> p r c", r=2)
        rstd = free[:, 16 * D + 16:16 * D + 18]
        mhalf = free[:, 16 * D + 18:16 * D + 19]
        a12 = adjT[:, 0, 0:4 * DH].bitcast(F32)
        wtmp = acc[:, 0, 0:D]

        bank = [ctx.enter_context(nc.psum_tensor(f"bank{k}", [P, 512], F32)) for k in range(8)]
        scratch = nc.dram_tensor("a_rows", [H, N], F32, kind="Internal")

        w_loaded, a12_loaded = sem("w_loaded"), sem("a12_loaded")
        x_loaded = [sem("x_loaded0"), sem("x_loaded1")]
        adj_loaded = [sem("adj_loaded0"), sem("adj_loaded1")]
        abc_loaded = [sem("abc_loaded0"), sem("abc_loaded1")]
        wo_loaded, bout_loaded, a_stored = sem("wo_loaded"), sem("bout_loaded"), sem("a_stored")
        xr_loaded = [sem("xr_loaded0"), sem("xr_loaded1")]
        stored = [sem("stored0"), sem("stored1")]
        ident0, ident = sem("ident0"), sem("ident")
        wa_steps, wa_ready = sem("wa_steps"), sem("wa_ready")
        x_turned, x_copied, seq_made, seq_copied = (sem(s) for s in ("x_turned", "x_copied", "seq_made", "seq_copied"))
        adj_cast, adj_fixed, adj_turned, adj_ready = (sem(s) for s in ("adj_cast", "adj_fixed", "adj_turned", "adj_ready"))
        noedge_set = sem("noedge_set")
        a_turned, a_copied = sem("a_turned"), sem("a_copied")
        dve_step = sem("dve_step")
        mx_turned, mx_spread = sem("mx_turned"), sem("mx_spread")
        e_in, e_out, r_in, r_out, e_scaled = (sem(s) for s in ("e_in", "e_out", "r_in", "r_out", "e_scaled"))
        ones_hi, xp_made, vp_hi, vp_ready = (sem(s) for s in ("ones_hi", "xp_made", "vp_hi", "vp_ready"))
        nbs_ready, acc_zero = sem("nbs_ready"), sem("acc_zero")
        u_ready, t_ready, t_free = sem("u_ready"), sem("t_ready"), sem("t_free")
        bank_done, hlo_ready, comb_ready, fin_done = (sem(s) for s in ("bank_done", "hlo_ready", "comb_ready", "fin_done"))
        adj_done, glo_ready, gsum_ready, gsum_used = (sem(s) for s in ("adj_done", "glo_ready", "gsum_ready", "gsum_used"))
        gsum_scaled, fin_step = sem("gsum_scaled"), sem("fin_step")
        rden_ready, hid_ready, h_turned, h_copied, z_made = (sem(s) for s in ("rden_ready", "hid_ready", "h_turned", "h_copied", "z_made"))
        z_ready, zmin_ready, e_ready, elu_ready, y_ready = (sem(s) for s in ("z_ready", "zmin_ready", "e_ready", "elu_ready", "y_ready"))
        stats_ready, mv_ready, v_eps, rstd_ready, out_ready = (sem(s) for s in ("stats_ready", "mv_ready", "v_eps", "rstd_ready", "out_ready"))
        gate, gate_dve = sem("gate"), sem("gate_dve")
        den_inv, mhalf_set = sem("den_inv"), sem("mhalf_set")

        block = ctx.enter_context(nc.Block())

        x_t = x.rearrange("(t p) d -> t p d", p=P)
        out_t = out.rearrange("(t p) d -> t p d", p=P)
        adj_t = adj.rearrange("(t p) n -> t p n", p=P)

        def live(i, lag):
            return not isinstance(i, int) or lag <= i < NT + lag

        def past(i, n):
            return not isinstance(i, int) or i >= n

        def over_tiles(eng, body):
            for i in range(4):
                body(i, i % 2)
            with eng.Fori(2, NT // 2) as k:
                for q in range(2):
                    body(2 * k + q, q)
            for i in (NT, NT + 1):
                body(i, i % 2)

        @block.sync
        def _(sp):
            sp.dma_start(W_sb, W_seq.rearrange("(k p) n -> p k n", p=P)).then_inc(w_loaded, 16)
            sp.dma_start(a12[:, 0:DH], a1.rearrange("(o d) -> o d", o=1).partition_broadcast(P)).then_inc(a12_loaded, 16)
            sp.dma_start(a12[:, DH:2 * DH], a2.rearrange("(o d) -> o d", o=1).partition_broadcast(P)).then_inc(a12_loaded, 16)

            def load_adj(it, r):
                sp.wait_ge(adj_cast, it + 1)
                sp.dma_start(stage[:, r, :], adj_t[it]).then_inc(adj_loaded[r], 16)

            with sp.Fori(0, NT // 4) as k:
                for u in range(4):
                    sp.wait_ge(x_turned, 4 * k + u + 1)
                    sp.dma_start(xs[:, u % 2, :], x_t[4 * k + u]).then_inc(x_loaded[u % 2], 16)
                    if u % 2:
                        load_adj(2 * k + u // 2, u // 2)
            sp.wait_ge(a_copied, 4)
            sp.dma_start(scratch[:, :], aT).then_inc(a_stored, 16)
            for q in range(2):
                load_adj(NT // 2 + q, q)
            sp.wait_ge(a_stored, 16)
            sp.dma_start(abc[:, 0, :], scratch[0:1, :].partition_broadcast(P)).then_inc(abc_loaded[0], 16)
            with sp.Fori(1, NT // 4) as k:
                for q in range(2):
                    load_adj(NT // 2 + 2 * k + q, q)
            sp.wait_ge(vp_ready, 2 + 2 * H)
            sp.dma_start(abc[:, 1, :], scratch[1:2, :].partition_broadcast(P)).then_inc(abc_loaded[1], 16)
            with sp.Fori(1, H // 2) as k:
                for q in range(2):
                    sp.wait_ge(t_ready, NT * (2 * k + q - 1))
                    sp.dma_start(abc[:, q, :], scratch[bass.ds(2 * k + q, 1), :].partition_broadcast(P)).then_inc(abc_loaded[q], 16)
            sp.wait_ge(t_ready, NT * (H - 1))
            sp.dma_start(Wo_sb, W_out.rearrange("(k p) n -> p k n", p=P)).then_inc(wo_loaded, 16)
            sp.wait_ge(t_free, RING + NT * H)
            sp.wait_ge(adj_done, STEPS * H)
            sp.dma_start(bout, b_out.rearrange("(o d) -> o d", o=1).partition_broadcast(P)).then_inc(bout_loaded, 16)

            def tail(i, r):
                if live(i, 0):
                    if past(i, 2):
                        sp.wait_ge(y_ready, i - 1)
                    sp.dma_start(xr[:, r, :], x_t[i]).then_inc(xr_loaded[r], 16)
                if live(i, 2):
                    sp.wait_ge(out_ready, i - 1)
                    sp.dma_start(out_t[i - 2], ot[:, r, :]).then_inc(stored[r], 16)

            over_tiles(sp, tail)
            for q in range(2):
                sp.wait_ge(stored[q], 16 * NT // 2)

        @block.tensor
        def _(pe):
            pe.sem_inc(x_turned, 2)
            pe.sem_inc(seq_made, 2)
            pe.sem_inc(adj_turned, 4)
            pe.sem_inc(t_free, RING)
            pe.wait_ge(ident, 2)

            def turn_x(t, r, n):
                pe.wait_ge(x_loaded[r], 16 * n)
                pe.wait_ge(x_copied, t + 1)
                for k in range(KT):
                    mm = pe.transpose(bank[r][:, k * P:(k + 1) * P], xs[:, r, k * P:(k + 1) * P], idf[:])
                mm.then_inc(x_turned, 1)

            def project(t, r):
                pe.wait_ge(x_copied, 2 + t + 1)
                pe.wait_ge(seq_copied, t + 1)
                for k in range(KT):
                    pe.matmul(bank[2 + r][:], xT[:, r, k * P:(k + 1) * P], W_sb[:, k, :],
                              start=(k == 0), stop=(k == KT - 1))
                for k in range(KT):
                    mm = pe.matmul(bank[4 + r][:, 0:2 * H], xT[:, r, k * P:(k + 1) * P], wa[:, k, :, :],
                                   start=(k == 0), stop=(k == KT - 1))
                mm.then_inc(seq_made, 1)

            def turn_adj(it, r):
                pe.wait_ge(adj_fixed, it + 1)
                for half in range(2):
                    pe.wait_ge(adj_ready, 2 * it + half + 1)
                    for q in range(8):
                        j = 8 * half + q
                        mm = pe.transpose(bank[6 + half][:].bitcast(BF16)[:, q * P:(q + 1) * P],
                                          adjb[:, r, j * P:(j + 1) * P], idb[:])
                    mm.then_inc(adj_turned, 1)

            turn_x(0, 0, 1)
            pe.wait_ge(w_loaded, 16)
            pe.wait_ge(wa_ready, 1)

            def x_steps(k, last):
                for u in range(4):
                    t = 4 * k + u
                    if not (last and u == 3):
                        turn_x(t + 1, (u + 1) % 2, 2 * k + (u + 1) // 2 + 1)
                    project(t, u % 2)
                    if u % 2:
                        turn_adj(2 * k + u // 2, u // 2)

            with pe.Fori(0, NT // 4 - 1) as k:
                x_steps(k, False)
            x_steps(NT // 4 - 1, True)

            pe.wait_ge(seq_copied, 2 + NT)
            for t in range(NT):
                mm = pe.transpose(bank[t // 4][0:H, t % 4 * P:(t % 4 + 1) * P], ab[:, t, 0:H], idf[:])
                if t % 4 == 3:
                    mm.then_inc(a_turned, 1)
            pe.wait_ge(dve_step, 3)
            pe.transpose(bank[4][0:2 * H, 0:P], mx, idf[:]).then_inc(mx_turned, 1)
            pe.wait_ge(dve_step, 5)
            pe.matmul(bank[5][:, 0:2 * H], ones[0:2 * H, :], diag[0:2 * H, :], start=True, stop=True).then_inc(mx_spread, 1)
            with pe.Fori(0, NT // 4) as k:
                for q in range(2):
                    turn_adj(NT // 2 + 2 * k + q, q)
            pe.wait_ge(adj_ready, 2 + 2 * NT)
            pe.wait_ge(vp_ready, 2 + 2 * H)

            def head(h, first):
                for jt in range(NT):
                    pe.wait_ge(t_ready, NT * h + jt + 1)
                    for it in range(NT):
                        b, c = it // ITB, it % ITB
                        if jt == 0 and c == 0 and not first:
                            pe.wait_ge(comb_ready, BANKS * h - BANKS + b + 1)
                        mm = pe.matmul(bank[b][:, c * 2 * VW:(c + 1) * 2 * VW],
                                       tring[:, jt % RING, it * P:(it + 1) * P], Vp[:, jt, h, :, :],
                                       start=(jt == 0 and c == 0), stop=(jt == NT - 1), skip_group_check=True)
                        if jt == NT - 1 and c == ITB - 1:
                            mm.then_inc(bank_done, 1)
                    mm.then_inc(t_free, 1)
                    if jt % RING == RING - 1:
                        u = jt // RING
                        if not (first and u < 2):
                            pe.wait_ge(gsum_ready, STEPS * h + u - 1)
                        it, g = STEPS * (h % GRP) + u, h // GRP
                        for j in range(NT):
                            mm = pe.matmul(bank[6 + u % 2][:, 0:GRP * 2 * HW], adjT[:, j, bass.ds(it * P, P)],
                                           Vp[:, j, bass.ds(GRP * g, GRP), :, COL_B:COL_A1],
                                           start=(j == 0), stop=(j == NT - 1))
                        mm.then_inc(adj_done, 1)

            head(0, True)
            with pe.Fori(1, H) as h:
                head(h, False)

            pe.wait_ge(comb_ready, BANKS * H)
            pe.wait_ge(gsum_ready, STEPS * H)
            pe.wait_ge(wo_loaded, 16)

            def tail(i, r):
                if live(i, 0):
                    pe.wait_ge(hid_ready, i + 1)
                    if past(i, 2):
                        pe.wait_ge(h_copied, i - 1)
                    for k in range(KT):
                        mm = pe.transpose(bank[r][:, k * P:(k + 1) * P], hid[:, r, k * P:(k + 1) * P], idf[:])
                    mm.then_inc(h_turned, 1)
                if live(i, 1):
                    q = 1 - r
                    pe.wait_ge(h_copied, i)
                    if past(i, 3):
                        pe.wait_ge(z_ready, i - 2)
                    for k in range(KT):
                        mm = pe.matmul(bank[2 + q][:], hT[:, q, k * P:(k + 1) * P], Wo_sb[:, k, :],
                                       start=(k == 0), stop=(k == KT - 1))
                    mm.then_inc(z_made, 1)

            over_tiles(pe, tail)

        @block.scalar
        def _(act):
            act.sem_inc(x_copied, 2)
            act.sem_inc(adj_cast, 2)

            def copy_x(t, r):
                act.wait_ge(x_turned, 2 + t + 1)
                act.wait_ge(seq_made, t + 1)
                act.copy(xT[:, r, :], bank[r][:]).then_inc(x_copied, 1)

            def cast_adj(it, r, n):
                act.wait_ge(adj_loaded[r], 16 * n)
                act.wait_ge(adj_turned, 2 * it + 2)
                act.activation(adjb[:, r, :], stage[:, r, :], ACT.Copy, accum_out=deg[:, r:r + 1]).then_inc(adj_cast, 1)

            with act.Fori(0, NT // 4) as k:
                for u in range(4):
                    copy_x(4 * k + u, u % 2)
                    if u % 2:
                        cast_adj(2 * k + u // 2, u // 2, k + 1)

            for c in range(4):
                act.wait_ge(a_turned, c + 1)
                act.copy(aT[:, c * 512:(c + 1) * 512], bank[c][0:H, :]).then_inc(a_copied, 1)
            act.wait_ge(e_in, 1)
            act.activation(E[:, :, 1, :], E[:, :, 0, :], ACT.Exp, scale=-SLOPE).then_inc(e_out, 1)
            act.wait_ge(e_out, 1)
            act.activation(E[:, :, 0, :], E[:, :, 0, :], ACT.Exp, scale=-1.0).then_inc(e_out, 1)
            act.wait_ge(r_in, 1)
            act.activation(ab[:, :, 0:H], ab[:, :, 0:H], ACT.Exp, scale=SLOPE - 1.0).then_inc(r_out, 1)
            act.wait_ge(e_out, 2)
            act.activation(Vp[:, :, :, 0, COL_A1], E[:, :, 0, :], ACT.Copy, scale=TOP).then_inc(ones_hi, 1)
            act.activation(Vp[:, :, :, 0, COL_B1], E[:, :, 1, :], ACT.Copy, scale=TOP).then_inc(ones_hi, 1)

            with act.Fori(0, NT // 4) as k:
                for q in range(2):
                    cast_adj(NT // 2 + 2 * k + q, q, NT // 4 + k + 1)
                    for v in range(2):
                        h = 4 * k + 2 * q + v
                        for s in range(2):
                            act.wait_ge(xp_made, 2 * h + s + 1)
                            act.activation(Vp[:, :, h, 0, s * DH:(s + 1) * DH], xp[s], ACT.Copy,
                                           scale=1.0 / LO).then_inc(vp_hi, 1)

            def bank_lows(h):
                for b in range(BANKS):
                    n = min(ITB, NT - b * ITB)
                    if n == ITB:
                        act.wait_ge(bank_done, (BANKS - 1) * (h - 1) + b + 1)
                    else:
                        act.wait_ge(t_free, RING + NT * h)
                    if not (isinstance(h, int) and h == 1 and b < 2):
                        act.wait_ge(comb_ready, BANKS * h - BANKS + b - 1)
                    lows = bank[b][:, 0:n * 2 * VW].rearrange("p (t s c) -> p t s c", s=2, c=VW)[:, :, 1, :]
                    act.activation(hlo[:, b % 2, 0:n, :], lows, ACT.Copy, scale=1.0 / LO).then_inc(hlo_ready, 1)

            def adj_low(s, r, early):
                act.wait_ge(adj_done, s + 1)
                if not early:
                    act.wait_ge(gsum_ready, s - 1)
                lows = bank[6 + r][:, 0:GRP * 2 * HW].rearrange("p (g s c) -> p g s c", s=2, c=HW)[:, :, 1, :]
                act.activation(glo[:, r, :, :], lows, ACT.Copy, scale=1.0 / LO).then_inc(glo_ready, 1)

            def head(h, par, n, first):
                act.wait_ge(abc_loaded[par], 16 * n)
                for jt in range(NT):
                    if jt % RING != RING - 1:
                        act.wait_ge(t_free, NT * h + jt + 1)
                        act.activation(tring[:, jt % RING, :], abc[:, par, :], ACT.Relu, bias=nbs[:, jt, bass.ds(h, 1)],
                                       scale=-SIGN_SCALE).then_inc(u_ready, 1)
                    if jt % RING == 1 and not (first and jt == 1):
                        u = jt // RING
                        adj_low(STEPS * h + u - 1, (u - 1) % 2, first and u < 3)
                        if jt == 1:
                            bank_lows(h)

            act.wait_ge(adj_cast, 2 + NT)
            act.wait_ge(adj_ready, 2 + 2 * NT)
            act.wait_ge(nbs_ready, 1)
            act.wait_ge(vp_ready, 2 + 2 * H)
            head(0, 0, 1, True)
            head(1, 1, 1, False)
            with act.Fori(1, H // 2) as k:
                for q in range(2):
                    head(2 * k + q, q, k + 1, False)
            adj_low(STEPS * H - 1, 1, False)
            bank_lows(H)

            def tail(i, r):
                if live(i, 0):
                    act.wait_ge(h_turned, i + 1)
                    if past(i, 2):
                        act.wait_ge(z_made, i - 1)
                    act.copy(hT[:, r, :], bank[r][:]).then_inc(h_copied, 1)
                if live(i, 1):
                    act.wait_ge(zmin_ready, i)
                    act.activation(et[:, 1 - r, :], et[:, 1 - r, :], ACT.Exp).then_inc(e_ready, 1)

            over_tiles(act, tail)

        @block.vector
        def _(dve):
            dve.wait_ge(w_loaded, 16)
            dve.wait_ge(a12_loaded, 32)
            n = 0
            for s in range(2):
                for k in range(KT):
                    if n:
                        dve.wait_ge(wa_steps, 2 * n)
                    dve.tensor_tensor(wtmp.rearrange("p (h d) -> p h d", h=H),
                                      W_sb[:, k, :].rearrange("p (h d) -> p h d", h=H),
                                      a12[:, s * DH:(s + 1) * DH].unsqueeze(1).to_broadcast([P, H, DH]),
                                      ALU.mult).then_inc(wa_steps, 1)
                    dve.wait_ge(wa_steps, 2 * n + 1)
                    ins = dve.tensor_reduce(wa[:, k, s, :], wtmp.rearrange("p (h d) -> p h d", h=H),
                                            AX.X, ALU.add)
                    ins.then_inc(wa_steps, 1)
                    n += 1
            dve.wait_ge(wa_steps, 2 * n)
            dve.sem_inc(wa_ready, 1)
            dve.sem_inc(seq_copied, 2)
            dve.sem_inc(adj_ready, 2)
            dve.sem_inc(vp_ready, 2)

            def copy_seq(t, r):
                dve.wait_ge(seq_made, 2 + t + 1)
                dve.tensor_copy(acc[:, t, 0:D], bank[2 + r][:])
                dve.tensor_reduce(nbs[:, t, :], bank[2 + r][:].rearrange("p (h d) -> p h d", h=H), AX.X, ALU.max,
                                  apply_absolute_value=True)
                dve.tensor_copy(ab[:, t, 0:H], bank[4 + r][:, 0:H])
                dve.tensor_scalar(ab[:, t, H:2 * H], bank[4 + r][:, H:2 * H], -1.0, None, ALU.mult).then_inc(seq_copied, 1)

            def fix_adj(it, r):
                dve.wait_ge(adj_cast, 2 + it + 1)
                dve.tensor_scalar(noedge[:, r:r + 1], deg[:, r:r + 1], 0.0, None, ALU.is_equal).then_inc(noedge_set, 1)
                dve.wait_ge(noedge_set, it + 1)
                dve.tensor_scalar(adjb[:, r, :], adjb[:, r, :], noedge[:, r:r + 1], None, ALU.max).then_inc(adj_fixed, 1)

            def copy_adj(it):
                for half in range(2):
                    dve.wait_ge(adj_turned, 4 + 2 * it + half + 1)
                    dve.tensor_copy(adjT[:, 8 * half:8 * half + 8, bass.ds(it * P, P)],
                                    bank[6 + half][:].bitcast(BF16).rearrange("p (j i) -> p j i", j=8)).then_inc(adj_ready, 1)

            with dve.Fori(0, NT // 4) as k:
                for u in range(4):
                    copy_seq(4 * k + u, u % 2)
                    if u % 2:
                        fix_adj(2 * k + u // 2, u // 2)
                        copy_adj(2 * k + u // 2)

            dve.wait_ge(seq_copied, 2 + NT)
            dve.memset(ones, 1.0).then_inc(dve_step, 1)
            dve.tensor_reduce(mx[:, 0:H], ab[:, :, H:2 * H].rearrange("p t h -> p h t"), AX.X, ALU.min,
                              negate=True).then_inc(dve_step, 1)
            dve.tensor_reduce(mx[:, H:2 * H], nbs[:].rearrange("p t h -> p h t"), AX.X, ALU.max).then_inc(dve_step, 1)
            dve.wait_ge(mx_turned, 1)
            dve.tensor_reduce(mcol[0:2 * H, :], bank[4][0:2 * H, 0:P], AX.X, ALU.max).then_inc(dve_step, 1)
            dve.wait_ge(dve_step, 4)
            dve.tensor_scalar(diag[0:2 * H, :], idf[0:2 * H, 0:2 * H], mcol[0:2 * H, :], None, ALU.mult).then_inc(dve_step, 1)
            dve.tensor_scalar(nbs[:], ab[:, :, H:2 * H], SIGN_SCALE, None, ALU.mult).then_inc(nbs_ready, 1)
            dve.wait_ge(mx_spread, 1)
            dve.tensor_copy(Mb[:], bank[5][:, 0:2 * H]).then_inc(dve_step, 1)
            dve.wait_ge(dve_step, 6)
            Mrow = Mb[:, 0:H].unsqueeze(1).to_broadcast([P, NT, H])
            dve.tensor_tensor(E[:, :, 0, :], ab[:, :, H:2 * H], Mrow, ALU.add).then_inc(e_in, 1)
            dve.wait_ge(a_turned, 4)
            dve.tensor_tensor(ab[:, :, 0:H], ab[:, :, 0:H], Mrow, ALU.add).then_inc(dve_step, 1)
            dve.wait_ge(dve_step, 7)
            dve.tensor_scalar(ab[:, :, 0:H], ab[:, :, 0:H], 0.0, None, ALU.max).then_inc(r_in, 1)
            dve.tensor_scalar(vsc[:], Mb[:, H:2 * H], TINY, None, ALU.max).then_inc(dve_step, 1)
            dve.wait_ge(dve_step, 8)
            dve.tensor_scalar(vsc[:].bitcast(U32), vsc[:].bitcast(U32), 0x7F800000, None, ALU.bitwise_and).then_inc(dve_step, 1)
            dve.wait_ge(dve_step, 9)
            dve.reciprocal(vinv[:], vsc[:]).then_inc(dve_step, 1)
            dve.wait_ge(dve_step, 10)
            dve.tensor_scalar(vinv[:], vinv[:], TOP * LO, None, ALU.mult).then_inc(dve_step, 1)
            dve.wait_ge(ones_hi, 2)
            dve.tensor_scalar(xp[0], E.rearrange("p t s h -> p t (s h)"), TOP * LO, None, ALU.mult).then_inc(dve_step, 1)
            dve.wait_ge(dve_step, 12)
            for s, col in ((0, COL_A1), (1, COL_B1)):
                dve.scalar_tensor_tensor(out=Vp[:, :, :, 1, col], in0=Vp[:, :, :, 0, col], scalar=-LO,
                                         in1=xp[0][:, :, s * H:(s + 1) * H], op0=ALU.mult, op1=ALU.add).then_inc(dve_step, 1)
            dve.wait_ge(dve_step, 14)
            dve.tensor_tensor(E.rearrange("p t s h -> p (t s) h"), E.rearrange("p t s h -> p (t s) h"),
                              vinv[:].unsqueeze(1).to_broadcast([P, 2 * NT, H]), ALU.mult).then_inc(e_scaled, 1)

            with dve.Fori(0, NT // 4) as k:
                for q in range(2):
                    fix_adj(NT // 2 + 2 * k + q, q)
                    for v in range(2):
                        h = 4 * k + 2 * q + v
                        for s in range(2):
                            dve.wait_ge(vp_hi, 2 * h + s + 1)
                            dve.scalar_tensor_tensor(out=Vp[:, :, h, 1, s * DH:(s + 1) * DH],
                                                     in0=Vp[:, :, h, 0, s * DH:(s + 1) * DH], scalar=-LO,
                                                     in1=xp[s], op0=ALU.mult, op1=ALU.add).then_inc(vp_ready, 1)
                    copy_adj(NT // 2 + 2 * k + q)

            def bank_sums(h):
                if not (isinstance(h, int) and h == 1):
                    dve.wait_ge(fin_done, h - 1)
                for b in range(BANKS):
                    n = min(ITB, NT - b * ITB)
                    dve.wait_ge(hlo_ready, BANKS * h - BANKS + b + 1)
                    highs = bank[b][:, 0:n * 2 * VW].rearrange("p (t s c) -> p t s c", s=2, c=VW)[:, :, 0, :]
                    dve.tensor_tensor(comb[:, b * ITB:b * ITB + n, :], highs, hlo[:, b % 2, 0:n, :],
                                      ALU.add).then_inc(comb_ready, 1)

            def adj_sum(s, r, early):
                dve.wait_ge(glo_ready, s + 1)
                if not early:
                    dve.wait_ge(gsum_used, s - 1)
                highs = bank[6 + r][:, 0:GRP * 2 * HW].rearrange("p (g s c) -> p g s c", s=2, c=HW)[:, :, 0, :]
                dve.tensor_tensor(gsum[:, r, :, :], highs, glo[:, r, :, :], ALU.add).then_inc(gsum_ready, 1)

            def head(h, par, n, first):
                dve.wait_ge(abc_loaded[par], 16 * n)
                for jt in range(NT):
                    slot = tring[:, jt % RING, :]
                    if jt % RING == RING - 1:
                        dve.wait_ge(t_free, NT * h + jt + 1)
                        dve.scalar_tensor_tensor(out=slot, in0=abc[:, par, :], scalar=ab[:, jt, bass.ds(h + H, 1)],
                                                 in1=adjT[:, jt, :], op0=ALU.is_gt, op1=ALU.mult).then_inc(t_ready, 1)
                    else:
                        dve.wait_ge(u_ready, ACT_PER_HEAD * h + jt - jt // RING + 1)
                        dve.tensor_tensor(slot, adjT[:, jt, :], slot, ALU.is_gt).then_inc(t_ready, 1)
                    if jt % RING == 1 and not (first and jt == 1):
                        u = jt // RING
                        adj_sum(STEPS * h + u - 1, (u - 1) % 2, first and u < 3)
                        if jt == 1:
                            bank_sums(h)

            dve.wait_ge(adj_ready, 2 + 2 * NT)
            head(0, 0, 1, True)
            head(1, 1, 1, False)
            with dve.Fori(1, H // 2) as k:
                for q in range(2):
                    head(2 * k + q, q, k + 1, False)
            adj_sum(STEPS * H - 1, 1, False)
            bank_sums(H)

            dve.wait_ge(fin_done, H)
            dve.wait_ge(gsum_used, STEPS * H)
            dens = acc[:].rearrange("p t (h c) -> p t h c", c=HW)[:, :, :, DH]
            dve.reciprocal(rden, dens).then_inc(den_inv, 1)
            dve.memset(mhalf, -0.5).then_inc(mhalf_set, 1)
            dve.wait_ge(den_inv, 1)
            dve.tensor_tensor(rden, rden, vsc[:].unsqueeze(1).to_broadcast([P, NT, H]), ALU.mult).then_inc(rden_ready, 1)
            dve.wait_ge(bout_loaded, 16)

            def tail(i, r):
                q = 1 - r
                if live(i, 0):
                    dve.wait_ge(z_made, i + 1)
                    dve.tensor_tensor(zt[:, r, :], bank[2 + r][:], bout, ALU.add).then_inc(z_ready, 1)
                    dve.wait_ge(z_ready, i + 1)
                    dve.tensor_scalar(et[:, r, :], zt[:, r, :], 0.0, None, ALU.min).then_inc(zmin_ready, 1)
                if live(i, 1):
                    dve.wait_ge(e_ready, i)
                    if past(i, 3):
                        dve.wait_ge(out_ready, i - 2)
                    dve.scalar_tensor_tensor(out=yt[:, q, :], in0=zt[:, q, :], scalar=0.0, in1=et[:, q, :],
                                             op0=ALU.max, op1=ALU.add).then_inc(elu_ready, 1)
                    dve.wait_ge(elu_ready, i)
                    dve.wait_ge(xr_loaded[q], 8 * (i + r))
                    dve.scalar_tensor_tensor(out=yt[:, q, :], in0=yt[:, q, :], scalar=-1.0, in1=xr[:, q, :],
                                             op0=ALU.add, op1=ALU.add).then_inc(y_ready, 1)
                    dve.wait_ge(y_ready, i)
                    dve.bn_stats(stats[:, q, :], yt[:, q, :]).then_inc(stats_ready, 1)
                    dve.wait_ge(stats_ready, i)
                    dve.sem_inc(gate_dve, 1)
                    dve.bn_aggr(mv[:, q, :], stats[:, q, :]).then_inc(mv_ready, 1)
                if live(i, 2):
                    dve.wait_ge(rstd_ready, i - 1)
                    if past(i, 4):
                        dve.wait_ge(stored[r], 8 * (i - r - 2))
                    dve.tensor_scalar(ot[:, r, :], yt[:, r, :], mv[:, r, 0:1], rstd[:, r:r + 1],
                                      ALU.subtract, ALU.mult).then_inc(out_ready, 1)

            over_tiles(dve, tail)

        @block.gpsimd
        def _(pool):
            pool.memset(idf[:], 0.0).then_inc(ident0, 1)
            pool.memset(idb[:], 0.0).then_inc(ident0, 1)
            pool.wait_ge(ident0, 2)
            for t in (idf, idb):
                pool.affine_select(out=t[:], in_=t[:], compare_op=ALU.not_equal, fill=1.0, base=0,
                                   pattern=[[-1, P]], channel_multiplier=1).then_inc(ident, 1)

            pool.wait_ge(e_scaled, 1)
            with pool.Fori(0, H) as h:
                for s in range(2):
                    pool.wait_ge(vp_ready, 2 * h + s + 1)
                    pool.sem_inc(gate, 1)
                    pool.tensor_tensor(xp[s], seq[:, :, bass.ds(h * DH, DH)],
                                       E[:, :, s, bass.ds(h, 1)].to_broadcast([P, NT, DH]), ALU.mult).then_inc(xp_made, 1)
            pool.wait_ge(xp_made, 2 * H)
            pool.memset(acc[:], 0.0).then_inc(acc_zero, 1)
            pool.wait_ge(acc_zero, 1)
            pool.wait_ge(r_out, 1)

            def adj_add(s, it, g, r):
                pool.wait_ge(gsum_ready, s + 1)
                pool.sem_inc(gate, 1)
                R = ab[:, bass.ds(it, 1), bass.ds(GRP * g, GRP)].rearrange("p t g -> p (t g)").unsqueeze(2).to_broadcast([P, GRP, HW])
                pool.tensor_tensor(gsum[:, r, :, :], gsum[:, r, :, :], R, ALU.mult).then_inc(gsum_scaled, 1)
                pool.wait_ge(gsum_scaled, s + 1)
                pool.sem_inc(gate, 1)
                part = acc[:, bass.ds(it, 1), bass.ds(GRP * HW * g, GRP * HW)].rearrange("p t (g c) -> p (t g) c", c=HW)
                pool.tensor_tensor(part, part, gsum[:, r, :, :], ALU.add).then_inc(gsum_used, 1)

            def head_add(h):
                pool.wait_ge(comb_ready, BANKS * h)
                pool.sem_inc(gate, 1)
                R = ab[:, :, bass.ds(h - 1, 1)].to_broadcast([P, NT, HW])
                cB = comb[:, :, COL_B:COL_A1]
                part = acc[:, :, bass.ds(HW * (h - 1), HW)]
                den = acc[:, :, bass.ds(HW * (h - 1) + DH, 1)]
                vals = acc[:, :, bass.ds(HW * (h - 1), DH)]
                pool.tensor_tensor(cB, cB, R, ALU.mult).then_inc(fin_step, 1)
                pool.wait_ge(gsum_used, STEPS * h)
                pool.sem_inc(gate, 1)
                pool.tensor_tensor(vals, vals, comb[:, :, 0:DH], ALU.add).then_inc(fin_step, 1)
                pool.tensor_tensor(den, den, comb[:, :, COL_A1:COL_A1 + 1], ALU.add).then_inc(fin_step, 1)
                pool.wait_ge(fin_step, 3 * h)
                pool.sem_inc(gate, 1)
                pool.tensor_tensor(part, part, cB, ALU.subtract).then_inc(fin_done, 1)

            def head(h, first):
                if not first:
                    s = STEPS * h - 1
                    adj_add(s, s % NT, s // NT, 1)
                    head_add(h)
                    pool.wait_ge(fin_done, h)
                    pool.sem_inc(gate, 1)
                for u in range(STEPS - 1):
                    adj_add(STEPS * h + u, STEPS * (h % GRP) + u, h // GRP, u % 2)

            head(0, True)
            with pool.Fori(1, H) as h:
                head(h, False)
            adj_add(STEPS * H - 1, NT - 1, GROUPS - 1, 1)
            head_add(H)

            pool.wait_ge(rden_ready, 1)
            pool.wait_ge(mhalf_set, 1)

            def tail(i, r):
                if live(i, 0):
                    if past(i, 2):
                        pool.wait_ge(h_turned, i - 1)
                    pool.sem_inc(gate, 1)
                    sums = acc[:, bass.ds(i, 1), :].rearrange("p t (h c) -> p (t h) c", c=HW)[:, :, 0:DH]
                    inv = rden[:, bass.ds(i, 1), :].rearrange("p t h -> p (t h)").unsqueeze(2).to_broadcast([P, H, DH])
                    pool.tensor_tensor(hid[:, r, :].rearrange("p (h d) -> p h d", h=H), sums, inv,
                                       ALU.mult).then_inc(hid_ready, 1)
                if live(i, 2):
                    pool.wait_ge(mv_ready, i - 1)
                    if past(i, 4):
                        pool.wait_ge(out_ready, i - 3)
                    pool.sem_inc(gate, 1)
                    pool.tensor_scalar(rstd[:, r:r + 1], mv[:, r, 1:2], EPS, None, ALU.add).then_inc(v_eps, 1)
                    pool.wait_ge(v_eps, i - 1)
                    pool.tensor_tensor(rstd[:, r:r + 1], rstd[:, r:r + 1], mhalf, ALU.pow).then_inc(rstd_ready, 1)

            over_tiles(pool, tail)


_INS = ["x", "adj", "L0_gnn_W_seq", "L0_gnn_a1", "L0_gnn_a2", "L0_gnn_W_out", "L0_gnn_b_out"]


def kernel(**inputs):
    import numpy as _np
    import concourse.bacc as _bacc
    from concourse import mybir as _mybir
    from concourse.bass_utils import run_bass_kernel_spmd as _run

    nc = _bacc.Bacc("TRN2", target_bir_lowering=False, num_devices=1)
    arrays, args = {}, []
    for name in _INS:
        a = _np.ascontiguousarray(inputs[name])
        arrays[f"in_{name}_dram"] = a
        args.append(nc.dram_tensor(f"in_{name}_dram", a.shape, _mybir.dt.from_np(a.dtype), kind="ExternalInput").ap())
    args.append(nc.dram_tensor("out_0_dram", (N, D), F32, kind="ExternalOutput").ap())
    gat_kernel(nc, *args)
    r = _run(nc, [arrays], core_ids=[0])
    return r.results[0]["out_0_dram"]
```

```python
from contextlib import ExitStack

import concourse.bass as bass
from concourse import mybir

F32 = mybir.dt.float32
F16 = mybir.dt.float16
BF16 = mybir.dt.bfloat16
U32 = mybir.dt.uint32
ALU = mybir.AluOpType
ACT = mybir.ActivationFunctionType
AX = mybir.AxisListType

P = 128
N, D, H, DH = 2048, 512, 16, 32
NT = N // P
KT = D // P
SLOPE = 0.2
EPS = 1e-5

HW = DH + 1
VW = 2 * HW
LO = 2.0 ** 11
TOP = 2.0 ** 13
SIGN_SCALE = 2.0 ** 60
TINY = 2.0 ** -100

RING = 4
GRP = 4
GROUPS = H // GRP
ITB = 3
BANKS = -(-NT // ITB)
STEPS = NT // RING
ADJ_EARLY = 12
ADJ_HEADS = (GROUPS * NT - ADJ_EARLY) // STEPS
DVE_TILES = (3, 7, 11, 15)
ACT_TILES = NT - len(DVE_TILES)
SUMS_AT = 0
ADJ_AT = 2
FINISH_AT = 3


def gat_kernel(nc, x, adj, W_seq, a1, a2, W_out, b_out, out):
    with ExitStack() as ctx:
        def sb(name, shape, dt):
            return ctx.enter_context(nc.sbuf_tensor(name, shape, dt))

        def sem(name):
            return ctx.enter_context(nc.semaphore(name))

        adjT = sb("adjT", [P, NT, N], BF16)
        Vp = sb("Vp", [P, NT, H, 2, VW], F16)
        acc = sb("acc", [P, NT, H * HW], F32)
        abc = sb("abc", [P, 2, N], F32)
        tring = sb("tring", [P, RING, N], BF16)
        o = 2 * NT * VW
        wide = sb("wide", [P, o + 2 * GRP * HW], F32)
        ab = sb("ab", [P, NT, 2 * H], F32)
        nbs = sb("nbs", [P, NT, H], F32)
        idf = sb("idf", [P, P], F32)
        vsc = sb("vsc", [P, H], F32)

        OFF = H * HW - D
        seq = acc[:, :, OFF:]
        W_sb = abc[:, 0, :].rearrange("p (k n) -> p k n", k=KT)
        xs = abc[:, 1, 0:2 * D].rearrange("p (r n) -> p r n", r=2)
        xT = abc[:, 1, 2 * D:4 * D].rearrange("p (r n) -> p r n", r=2)
        aT = abc[0:H, 0, :]
        E = abc[:, 1, 0:2 * NT * H].rearrange("p (t s h) -> p t s h", t=NT, s=2)
        elo = abc[:, 1, 2 * NT * H:4 * NT * H].rearrange("p (t c) -> p t c", t=NT)
        misc = abc[:, 1, 4 * NT * H:N]
        mx, diag, ones, mcol = misc[:, 0:32], misc[:, 32:64], misc[:, 64:64 + P], misc[:, 200:201]
        Mb = misc[:, 208:208 + 2 * H]
        vinv = misc[:, 240:240 + H]
        tring32 = tring[:].rearrange("p r n -> p (r n)").bitcast(F32)
        stage = tring32.rearrange("p (r n) -> p r n", r=2)
        xp = [[tring32[:, (2 * s + r) * NT * DH:(2 * s + r + 1) * NT * DH].rearrange("p (t d) -> p t d", t=NT)
               for r in range(2)] for s in range(2)]
        wa = acc[:, 0:2 * KT, 0:OFF].rearrange("p (k s) h -> p k s h", s=2)
        adjb = wide[:, 0:N].bitcast(BF16).rearrange("p (r n) -> p r n", r=2)
        raw = wide[:, 0:o].rearrange("p (t s c) -> p t s c", s=2, c=VW)
        comb = raw[:, :, 0, :]
        glo = wide[:, o:].rearrange("p (r g c) -> p r g c", r=2, g=GRP)
        before = Vp[:].rearrange("p t h s c -> p (t h s c)")
        idb = before[:, 0:P].bitcast(BF16)
        deg, noedge = before[:, P:P + 4].bitcast(F32), before[:, P + 4:P + 8].bitcast(F32)

        Wo_sb = abc[:, 0, :].rearrange("p (k n) -> p k n", k=KT)
        free = Vp[:].rearrange("p t h s c -> p (t h s c)").bitcast(F32)

        def ring(k):
            return free[:, 2 * k * D:2 * (k + 1) * D].rearrange("p (r n) -> p r n", r=2)
        xr, hT, zt, et, yt, ot = (ring(k) for k in range(6))
        HID = 4
        hid = free[:, 18 * D:(18 + HID) * D].rearrange("p (r n) -> p r n", r=HID)
        bout = free[:, 14 * D:15 * D]
        rden = free[:, 15 * D:15 * D + NT * H].rearrange("p (t h) -> p t h", t=NT)
        stats = free[:, 16 * D:16 * D + 12].rearrange("p (r c) -> p r c", r=2)
        mv = free[:, 16 * D + 12:16 * D + 16].rearrange("p (r c) -> p r c", r=2)
        rstd = free[:, 16 * D + 16:16 * D + 18]
        mhalf = free[:, 16 * D + 18:16 * D + 19]
        a12 = adjT[:, 0, 0:4 * DH].bitcast(F32)
        wtmp = [acc[:, (2 + r) * KT:(3 + r) * KT, OFF:].rearrange("p k (h d) -> p k h d", h=H) for r in range(2)]

        bank = [ctx.enter_context(nc.psum_tensor(f"bank{k}", [P, 512], F32)) for k in range(8)]
        scratch = nc.dram_tensor("a_rows", [H, N], F32, kind="Internal")

        w_loaded, a12_loaded = sem("w_loaded"), sem("a12_loaded")
        x_loaded = [sem("x_loaded0"), sem("x_loaded1")]
        adj_loaded = [sem("adj_loaded0"), sem("adj_loaded1")]
        abc_loaded = sem("abc_loaded")
        wo_loaded, bout_loaded, a_stored = sem("wo_loaded"), sem("bout_loaded"), sem("a_stored")
        xr_loaded = [sem("xr_loaded0"), sem("xr_loaded1")]
        stored = [sem("stored0"), sem("stored1")]
        ident0, ident = sem("ident0"), sem("ident")
        wa_prod, wa_ready = [sem("wa_prod1"), sem("wa_prod2")], sem("wa_ready")
        x_turned, x_copied, seq_made, seq_copied = (sem(s) for s in ("x_turned", "x_copied", "seq_made", "seq_copied"))
        adj_cast, adj_fixed, adj_turned, adj_ready = (sem(s) for s in ("adj_cast", "adj_fixed", "adj_turned", "adj_ready"))
        noedge_set = sem("noedge_set")
        a_turned, a_copied = sem("a_turned"), sem("a_copied")
        dve_step = sem("dve_step")
        mx_turned, mx_spread = sem("mx_turned"), sem("mx_spread")
        e_in, e_out, r_in, r_out, e_scaled = (sem(s) for s in ("e_in", "e_out", "r_in", "r_out", "e_scaled"))
        ones_hi, vp_ready = sem("ones_hi"), sem("vp_ready")
        xp_made = [sem("xp_made_a"), sem("xp_made_b")]
        vp_hi = [sem("vp_hi_a"), sem("vp_hi_b")]
        xp_read, nbs_ready = sem("xp_read"), sem("nbs_ready")
        u_ready, t_ready, t_free = sem("u_ready"), sem("t_ready"), sem("t_free")
        bank_done, sums_copied, comb_ready, fin_done = (sem(s) for s in ("bank_done", "sums_copied", "comb_ready", "fin_done"))
        adj_done, glo_ready, gsum_ready = (sem(s) for s in ("adj_done", "glo_ready", "gsum_ready"))
        fin_sub, fin_mul = sem("fin_sub"), sem("fin_mul")
        rden_ready, hid_ready, h_turned, h_copied, z_made = (sem(s) for s in ("rden_ready", "hid_ready", "h_turned", "h_copied", "z_made"))
        z_ready, zmin_ready, e_ready, elu_ready, y_ready = (sem(s) for s in ("z_ready", "zmin_ready", "e_ready", "elu_ready", "y_ready"))
        stats_ready, mv_ready, v_eps, rstd_ready, out_ready = (sem(s) for s in ("stats_ready", "mv_ready", "v_eps", "rstd_ready", "out_ready"))
        gate, gate_dve, gate_sp = sem("gate"), sem("gate_dve"), sem("gate_sp")
        den_inv, mhalf_set = sem("den_inv"), sem("mhalf_set")

        block = ctx.enter_context(nc.Block())

        x_t = x.rearrange("(t p) d -> t p d", p=P)
        out_t = out.rearrange("(t p) d -> t p d", p=P)
        adj_t = adj.rearrange("(t p) n -> t p n", p=P)

        def live(i, lag):
            return not isinstance(i, int) or lag <= i < NT + lag

        def past(i, n):
            return not isinstance(i, int) or i >= n

        def over_tiles(eng, body, slots=2):
            for i in range(4):
                body(i, i % slots)
            with eng.Fori(4 // slots, NT // slots) as k:
                for q in range(slots):
                    body(slots * k + q, q)
            for i in (NT, NT + 1):
                body(i, i % slots)

        @block.sync
        def _(sp):
            sp.dma_start(W_sb, W_seq.rearrange("(k p) n -> p k n", p=P)).then_inc(w_loaded, 16)
            sp.dma_start(a12[:, 0:DH], a1.rearrange("(o d) -> o d", o=1).partition_broadcast(P)).then_inc(a12_loaded, 16)
            sp.dma_start(a12[:, DH:2 * DH], a2.rearrange("(o d) -> o d", o=1).partition_broadcast(P)).then_inc(a12_loaded, 16)

            with sp.Fori(0, NT // 2) as k:
                for r in range(2):
                    t = 2 * k + r
                    sp.wait_ge(x_turned, t + 1)
                    sp.dma_start(xs[:, r, :], x_t[t]).then_inc(x_loaded[r], 16)
                    sp.wait_ge(adj_cast, t + 1)
                    sp.dma_start(stage[:, r, :], adj_t[t]).then_inc(adj_loaded[r], 16)
            sp.wait_ge(a_copied, 4)
            sp.dma_start(scratch[:, :], aT).then_inc(a_stored, 16)
            sp.wait_ge(a_stored, 16)
            sp.dma_start(abc[:, 0, :], scratch[0:1, :].partition_broadcast(P)).then_inc(abc_loaded, 16)
            sp.wait_ge(abc_loaded, 16)
            sp.wait_ge(vp_ready, 2 + H)
            sp.dma_start(abc[:, 1, :], scratch[1:2, :].partition_broadcast(P)).then_inc(abc_loaded, 16)
            with sp.Fori(1, H // 2) as k:
                for r in range(2):
                    h = 2 * k + r
                    sp.wait_ge(abc_loaded, 16 * h)
                    sp.sem_inc(gate_sp, 1)
                    sp.wait_ge(t_ready, NT * h - NT)
                    sp.dma_start(abc[:, r, :], scratch[bass.ds(h, 1), :].partition_broadcast(P)).then_inc(abc_loaded, 16)
            sp.wait_ge(t_ready, NT * (H - 1))
            sp.dma_start(Wo_sb, W_out.rearrange("(k p) n -> p k n", p=P)).then_inc(wo_loaded, 16)
            sp.wait_ge(t_free, RING + NT * H)
            sp.wait_ge(fin_done, 1 + H)
            sp.dma_start(bout, b_out.rearrange("(o d) -> o d", o=1).partition_broadcast(P)).then_inc(bout_loaded, 16)

            def tail(i, r):
                if live(i, 0):
                    if past(i, 2):
                        sp.wait_ge(y_ready, i - 1)
                    sp.dma_start(xr[:, r, :], x_t[i]).then_inc(xr_loaded[r], 16)
                if live(i, 2):
                    sp.wait_ge(out_ready, i - 1)
                    sp.dma_start(out_t[i - 2], ot[:, r, :]).then_inc(stored[r], 16)

            over_tiles(sp, tail)
            for q in range(2):
                sp.wait_ge(stored[q], 16 * NT // 2)

        @block.tensor
        def _(pe):
            pe.sem_inc(x_turned, 2)
            pe.sem_inc(seq_made, 2)
            pe.sem_inc(adj_turned, 4)
            pe.sem_inc(t_free, RING)
            pe.wait_ge(ident, 2)

            def turn_x(t, r, n):
                pe.wait_ge(x_loaded[r], 16 * n)
                pe.wait_ge(x_copied, t + 1)
                for k in range(KT):
                    mm = pe.transpose(bank[r][:, k * P:(k + 1) * P], xs[:, r, k * P:(k + 1) * P], idf[:])
                mm.then_inc(x_turned, 1)

            def project(t, r):
                pe.wait_ge(x_copied, 2 + t + 1)
                pe.wait_ge(seq_copied, t + 1)
                for k in range(KT):
                    pe.matmul(bank[2 + r][:], xT[:, r, k * P:(k + 1) * P], W_sb[:, k, :],
                              start=(k == 0), stop=(k == KT - 1))
                pe.wait_ge(wa_ready, 2)
                for k in range(KT):
                    mm = pe.matmul(bank[4 + r][:, 0:2 * H], xT[:, r, k * P:(k + 1) * P], wa[:, k, :, :],
                                   start=(k == 0), stop=(k == KT - 1))
                mm.then_inc(seq_made, 1)

            def turn_adj(it, r):
                pe.wait_ge(adj_fixed, it + 1)
                for half in range(2):
                    pe.wait_ge(adj_ready, 2 * it + half + 1)
                    for q in range(8):
                        j = 8 * half + q
                        mm = pe.transpose(bank[6 + half][:].bitcast(BF16)[:, q * P:(q + 1) * P],
                                          adjb[:, r, j * P:(j + 1) * P], idb)
                    mm.then_inc(adj_turned, 1)

            turn_x(0, 0, 1)
            pe.wait_ge(w_loaded, 16)
            with pe.Fori(0, NT // 2 - 1) as k:
                for r in range(2):
                    turn_x(2 * k + r + 1, 1 - r, k + 1 + r)
                    project(2 * k + r, r)
                    turn_adj(2 * k + r, r)
            turn_x(NT - 1, 1, NT // 2)
            project(NT - 2, 0)
            turn_adj(NT - 2, 0)
            project(NT - 1, 1)
            turn_adj(NT - 1, 1)

            pe.wait_ge(seq_copied, 2 + NT)
            for t in range(NT):
                mm = pe.transpose(bank[t // 4][0:H, t % 4 * P:(t % 4 + 1) * P], ab[:, t, 0:H], idf[:])
                if t % 4 == 3:
                    mm.then_inc(a_turned, 1)
            pe.wait_ge(dve_step, 3)
            pe.transpose(bank[4][0:2 * H, 0:P], mx, idf[:]).then_inc(mx_turned, 1)
            pe.wait_ge(dve_step, 5)
            pe.matmul(bank[5][:, 0:2 * H], ones[0:2 * H, :], diag[0:2 * H, :], start=True, stop=True).then_inc(mx_spread, 1)
            pe.wait_ge(adj_ready, 2 + 2 * NT)
            pe.wait_ge(a_copied, 4)

            def adj_product(r, it, g, js):
                for j in js:
                    mm = pe.matmul(bank[6 + r][:, 0:GRP * 2 * HW], adjT[:, j, bass.ds(it * P, P)],
                                   Vp[:, j, bass.ds(GRP * g, GRP), :, HW:VW], start=(j == 0), stop=(j == NT - 1))
                if j == NT - 1:
                    mm.then_inc(adj_done, 1)

            pe.wait_ge(vp_ready, 2 + GRP)
            with pe.Fori(0, ADJ_EARLY // 2) as k:
                for r in range(2):
                    pe.wait_ge(gsum_ready, 2 * k + r + 1)
                    adj_product(r, 2 * k + r, 0, range(NT))
            pe.wait_ge(vp_ready, 2 + H)

            def head(h, first, with_adj):
                for jt in range(NT):
                    u = jt // RING
                    pe.wait_ge(t_ready, NT * h + jt + 1)
                    for it in range(NT):
                        b, c = it // ITB, it % ITB
                        if jt == 0 and c == 0 and not first:
                            pe.wait_ge(sums_copied, BANKS * h - BANKS + b + 1)
                        mm = pe.matmul(bank[b][:, c * 2 * VW:(c + 1) * 2 * VW],
                                       tring[:, jt % RING, it * P:(it + 1) * P], Vp[:, jt, h, :, :],
                                       start=(jt == 0 and c == 0), stop=(jt == NT - 1), skip_group_check=True)
                        if jt == NT - 1 and c == ITB - 1:
                            mm.then_inc(bank_done, 1)
                    mm.then_inc(t_free, 1)
                    if with_adj:
                        s = ADJ_EARLY + STEPS * h + u
                        if jt % RING == 0:
                            pe.wait_ge(gsum_ready, s + 1)
                        q = jt % RING
                        adj_product(u % 2, s % NT, s // NT, range(q * STEPS, (q + 1) * STEPS))

            head(0, True, True)
            with pe.Fori(1, ADJ_HEADS) as h:
                head(h, False, True)
            with pe.Fori(ADJ_HEADS, H) as h:
                head(h, False, False)

            pe.wait_ge(sums_copied, BANKS * H)
            pe.wait_ge(wo_loaded, 16)

            def tail(i, slot):
                r = slot % 2
                if live(i, 0):
                    pe.wait_ge(hid_ready, i + 1)
                    if past(i, 2):
                        pe.wait_ge(h_copied, i - 1)
                    for k in range(KT):
                        mm = pe.transpose(bank[r][:, k * P:(k + 1) * P], hid[:, slot, k * P:(k + 1) * P], idf[:])
                    mm.then_inc(h_turned, 1)
                if live(i, 1):
                    q = 1 - r
                    pe.wait_ge(h_copied, i)
                    if past(i, 3):
                        pe.wait_ge(z_ready, i - 2)
                    for k in range(KT):
                        mm = pe.matmul(bank[2 + q][:], hT[:, q, k * P:(k + 1) * P], Wo_sb[:, k, :],
                                       start=(k == 0), stop=(k == KT - 1))
                    mm.then_inc(z_made, 1)

            over_tiles(pe, tail, HID)

        @block.scalar
        def _(act):
            act.sem_inc(x_copied, 2)
            act.sem_inc(adj_cast, 2)

            def copy_x(t, r):
                act.wait_ge(x_turned, 2 + t + 1)
                act.wait_ge(seq_made, t + 1)
                act.copy(xT[:, r, :], bank[r][:]).then_inc(x_copied, 1)

            def cast_adj(it, r, n):
                act.wait_ge(adj_loaded[r], 16 * n)
                act.wait_ge(adj_turned, 2 * it + 2)
                act.activation(adjb[:, r, :], stage[:, r, :], ACT.Copy, accum_out=deg[:, r:r + 1]).then_inc(adj_cast, 1)

            with act.Fori(0, NT // 2) as k:
                for r in range(2):
                    copy_x(2 * k + r, r)
                    cast_adj(2 * k + r, r, k + 1)

            for c in range(4):
                act.wait_ge(a_turned, c + 1)
                act.copy(aT[:, c * 512:(c + 1) * 512], bank[c][0:H, :]).then_inc(a_copied, 1)
            act.wait_ge(e_in, 1)
            act.activation(E[:, :, 1, :], E[:, :, 0, :], ACT.Exp, scale=-SLOPE).then_inc(e_out, 1)
            act.wait_ge(e_out, 1)
            act.activation(E[:, :, 0, :], E[:, :, 0, :], ACT.Exp, scale=-1.0).then_inc(e_out, 1)
            act.wait_ge(r_in, 1)
            act.activation(ab[:, :, 0:H], ab[:, :, 0:H], ACT.Exp, scale=SLOPE - 1.0).then_inc(r_out, 1)
            act.wait_ge(e_out, 2)
            act.activation(Vp[:, :, :, 0, DH], E[:, :, 0, :], ACT.Copy, scale=TOP).then_inc(ones_hi, 1)
            act.activation(Vp[:, :, :, 0, HW + DH], E[:, :, 1, :], ACT.Copy, scale=TOP).then_inc(ones_hi, 1)

            def adj_low(s, r):
                act.wait_ge(adj_done, s + 1)
                act.wait_ge(gsum_ready, s + 1)
                lows = bank[6 + r][:, 0:GRP * 2 * HW].rearrange("p (g s c) -> p g s c", s=2, c=HW)[:, :, 1, :]
                act.activation(glo[:, r, :, :], lows, ACT.Copy, scale=1.0 / LO).then_inc(glo_ready, 1)

            def split_high(h, r):
                for s in range(2):
                    act.wait_ge(xp_made[s], h + 1)
                    act.activation(Vp[:, :, h, 0, s * HW:s * HW + DH], xp[s][r], ACT.Copy,
                                   scale=1.0 / LO).then_inc(vp_hi[s], 1)

            with act.Fori(0, GRP // 2) as k:
                for r in range(2):
                    split_high(2 * k + r, r)
            act.wait_ge(adj_ready, 2 + 2 * NT)
            with act.Fori(0, (H - GRP) // 2) as k:
                for r in range(2):
                    split_high(GRP + 2 * k + r, r)
                for r in range(2):
                    adj_low(2 * k + r, r)

            def copy_sums(h):
                act.wait_ge(fin_done, h)
                for b in range(BANKS):
                    n = min(ITB, NT - b * ITB)
                    if n == ITB:
                        act.wait_ge(bank_done, (BANKS - 1) * (h - 1) + b + 1)
                    else:
                        act.wait_ge(t_free, RING + NT * h)
                    act.activation(raw[:, b * ITB:b * ITB + n, :, :].rearrange("p t s c -> p (t s c)"),
                                   bank[b][:, 0:n * 2 * VW], ACT.Copy).then_inc(sums_copied, 1)

            def head(h, first, adj_before, with_adj):
                act.wait_ge(abc_loaded, 16 * h + 16)
                row = abc[:, bass.ds(h % 2, 1), :].rearrange("p o n -> p (o n)")
                for jt in range(NT):
                    if jt not in DVE_TILES:
                        act.wait_ge(t_free, NT * h + jt + 1)
                        act.activation(tring[:, jt % RING, :], row, ACT.Relu, bias=nbs[:, jt, bass.ds(h, 1)],
                                       scale=-SIGN_SCALE).then_inc(u_ready, 1)
                    if jt == SUMS_AT and not first:
                        copy_sums(h)
                    if jt % RING == ADJ_AT:
                        u = jt // RING
                        if adj_before if jt < RING else with_adj:
                            adj_low(ADJ_EARLY + STEPS * h + u - 1, (u - 1) % 2)

            act.wait_ge(vp_ready, 2 + H)
            head(0, True, False, True)
            with act.Fori(1, ADJ_HEADS) as h:
                head(h, False, True, True)
            head(ADJ_HEADS, False, True, False)
            with act.Fori(ADJ_HEADS + 1, H) as h:
                head(h, False, False, False)
            copy_sums(H)

            def tail(i, r):
                if live(i, 0):
                    act.wait_ge(h_turned, i + 1)
                    if past(i, 2):
                        act.wait_ge(z_made, i - 1)
                    act.copy(hT[:, r, :], bank[r][:]).then_inc(h_copied, 1)
                if live(i, 1):
                    act.wait_ge(zmin_ready, i)
                    act.activation(et[:, 1 - r, :], et[:, 1 - r, :], ACT.Exp).then_inc(e_ready, 1)

            over_tiles(act, tail)

        @block.vector
        def _(dve):
            dve.wait_ge(w_loaded, 16)
            dve.wait_ge(a12_loaded, 32)
            dve.tensor_tensor(wtmp[0], W_sb.rearrange("p k (h d) -> p k h d", h=H),
                              a12[:, 0:DH].unsqueeze(1).unsqueeze(1).to_broadcast([P, KT, H, DH]), ALU.mult).then_inc(wa_prod[0], 1)
            for r in range(2):
                dve.wait_ge(wa_prod[r], 1)
                dve.tensor_reduce(wa[:, :, r, :], wtmp[r], AX.X, ALU.add).then_inc(wa_ready, 1)
            dve.sem_inc(seq_copied, 2)
            dve.sem_inc(adj_ready, 2)
            dve.sem_inc(vp_ready, 2)
            dve.sem_inc(xp_read, 2)
            dve.sem_inc(gsum_ready, 2)
            dve.sem_inc(fin_done, 1)

            def copy_seq(t, r):
                dve.wait_ge(seq_made, 2 + t + 1)
                dve.tensor_copy(seq[:, t, :], bank[2 + r][:])
                dve.tensor_reduce(nbs[:, t, :], bank[2 + r][:].rearrange("p (h d) -> p h d", h=H), AX.X, ALU.max,
                                  apply_absolute_value=True)
                dve.tensor_copy(ab[:, t, 0:H], bank[4 + r][:, 0:H])
                dve.tensor_scalar(ab[:, t, H:2 * H], bank[4 + r][:, H:2 * H], -1.0, None, ALU.mult).then_inc(seq_copied, 1)

            def fix_adj(it, r):
                dve.wait_ge(adj_cast, 2 + it + 1)
                dve.tensor_scalar(noedge[:, r:r + 1], deg[:, r:r + 1], 0.0, None, ALU.is_equal).then_inc(noedge_set, 1)
                dve.wait_ge(noedge_set, it + 1)
                dve.tensor_scalar(adjb[:, r, :], adjb[:, r, :], noedge[:, r:r + 1], None, ALU.max).then_inc(adj_fixed, 1)

            def copy_adj(it):
                for half in range(2):
                    dve.wait_ge(adj_turned, 4 + 2 * it + half + 1)
                    dve.tensor_copy(adjT[:, 8 * half:8 * half + 8, bass.ds(it * P, P)],
                                    bank[6 + half][:].bitcast(BF16).rearrange("p (j i) -> p j i", j=8)).then_inc(adj_ready, 1)

            with dve.Fori(0, NT // 2) as k:
                for r in range(2):
                    fix_adj(2 * k + r, r)
                    copy_seq(2 * k + r, r)
                    copy_adj(2 * k + r)

            dve.wait_ge(seq_copied, 2 + NT)
            dve.memset(ones, 1.0).then_inc(dve_step, 1)
            dve.tensor_reduce(mx[:, 0:H], ab[:, :, H:2 * H].rearrange("p t h -> p h t"), AX.X, ALU.min,
                              negate=True).then_inc(dve_step, 1)
            dve.tensor_reduce(mx[:, H:2 * H], nbs[:].rearrange("p t h -> p h t"), AX.X, ALU.max).then_inc(dve_step, 1)
            dve.wait_ge(mx_turned, 1)
            dve.tensor_reduce(mcol[0:2 * H, :], bank[4][0:2 * H, 0:P], AX.X, ALU.max).then_inc(dve_step, 1)
            dve.wait_ge(dve_step, 4)
            dve.tensor_scalar(diag[0:2 * H, :], idf[0:2 * H, 0:2 * H], mcol[0:2 * H, :], None, ALU.mult).then_inc(dve_step, 1)
            dve.tensor_scalar(nbs[:], ab[:, :, H:2 * H], SIGN_SCALE, None, ALU.mult).then_inc(nbs_ready, 1)
            dve.wait_ge(mx_spread, 1)
            dve.tensor_copy(Mb, bank[5][:, 0:2 * H]).then_inc(dve_step, 1)
            dve.wait_ge(dve_step, 6)
            Mrow = Mb[:, 0:H].unsqueeze(1).to_broadcast([P, NT, H])
            dve.tensor_tensor(E[:, :, 0, :], ab[:, :, H:2 * H], Mrow, ALU.add).then_inc(e_in, 1)
            dve.wait_ge(a_turned, 4)
            dve.tensor_tensor(ab[:, :, 0:H], ab[:, :, 0:H], Mrow, ALU.add).then_inc(dve_step, 1)
            dve.wait_ge(dve_step, 7)
            dve.tensor_scalar(ab[:, :, 0:H], ab[:, :, 0:H], 0.0, None, ALU.max).then_inc(r_in, 1)
            dve.tensor_scalar(vsc[:], Mb[:, H:2 * H], TINY, None, ALU.max).then_inc(dve_step, 1)
            dve.wait_ge(dve_step, 8)
            dve.tensor_scalar(vsc[:].bitcast(U32), vsc[:].bitcast(U32), 0x7F800000, None, ALU.bitwise_and).then_inc(dve_step, 1)
            dve.wait_ge(dve_step, 9)
            dve.reciprocal(vinv, vsc[:]).then_inc(dve_step, 1)
            dve.wait_ge(dve_step, 10)
            dve.tensor_scalar(vinv, vinv, TOP * LO, None, ALU.mult).then_inc(dve_step, 1)
            dve.wait_ge(ones_hi, 2)
            dve.tensor_scalar(elo, E.rearrange("p t s h -> p t (s h)"), TOP * LO, None, ALU.mult).then_inc(dve_step, 1)
            dve.wait_ge(dve_step, 12)
            for s, col in ((0, DH), (1, HW + DH)):
                dve.scalar_tensor_tensor(out=Vp[:, :, :, 1, col], in0=Vp[:, :, :, 0, col], scalar=-LO,
                                         in1=elo[:, :, s * H:(s + 1) * H], op0=ALU.mult, op1=ALU.add).then_inc(dve_step, 1)
            dve.wait_ge(dve_step, 14)
            dve.tensor_tensor(E.rearrange("p t s h -> p (t s) h"), E.rearrange("p t s h -> p (t s) h"),
                              vinv.unsqueeze(1).to_broadcast([P, 2 * NT, H]), ALU.mult).then_inc(e_scaled, 1)

            dve.wait_ge(e_scaled, 1)
            def adj_sum(s, r, it, g):
                dve.wait_ge(glo_ready, s + 1)
                highs = bank[6 + r][:, 0:GRP * 2 * HW].rearrange("p (g s c) -> p g s c", s=2, c=HW)[:, :, 0, :]
                sums = acc[:, bass.ds(it, 1), bass.ds(GRP * HW * g, GRP * HW)].rearrange("p t (g c) -> p (t g) c", c=HW)
                dve.tensor_tensor(sums, highs, glo[:, r, :, :], ALU.add).then_inc(gsum_ready, 1)

            def split(first_head):
                for r in range(2):
                    h = first_head + r
                    dve.wait_ge(vp_ready, h + 1)
                    dve.tensor_tensor(xp[1][r], seq[:, :, bass.ds(h * DH, DH)],
                                      E[:, :, 1, bass.ds(h, 1)].to_broadcast([P, NT, DH]), ALU.mult).then_inc(xp_made[1], 1)
                for r in range(2):
                    h = first_head + r
                    for s in range(2):
                        dve.wait_ge(vp_hi[s], h + 1)
                        dve.scalar_tensor_tensor(out=Vp[:, :, h, 1, s * HW:s * HW + DH],
                                                 in0=Vp[:, :, h, 0, s * HW:s * HW + DH], scalar=-LO,
                                                 in1=xp[s][r], op0=ALU.mult, op1=ALU.add).then_inc((xp_read, vp_ready)[s], 1)

            with dve.Fori(0, GRP // 2) as k:
                split(2 * k)
            with dve.Fori(0, (H - GRP) // 2) as k:
                split(GRP + 2 * k)
                for r in range(2):
                    adj_sum(2 * k + r, r, 2 * k + r, 0)

            def finish_head(h, step):
                sums = acc[:, :, bass.ds(HW * (h - 1), HW)]
                cA, cB = comb[:, :, 0:HW], comb[:, :, HW:VW]
                if step == 0:
                    dve.wait_ge(sums_copied, BANKS * h)
                    dve.scalar_tensor_tensor(out=comb, in0=raw[:, :, 1, :], scalar=1.0 / LO, in1=comb,
                                             op0=ALU.mult, op1=ALU.add).then_inc(comb_ready, 1)
                if step == 1:
                    dve.wait_ge(comb_ready, h)
                    dve.tensor_tensor(cB, sums, cB, ALU.subtract).then_inc(fin_sub, 1)
                if step == 2:
                    dve.wait_ge(fin_sub, h)
                    R = ab[:, :, bass.ds(h - 1, 1)].to_broadcast([P, NT, HW])
                    dve.tensor_tensor(cB, cB, R, ALU.mult).then_inc(fin_mul, 1)
                if step == 3:
                    dve.wait_ge(fin_mul, h)
                    dve.tensor_tensor(sums, cA, cB, ALU.add).then_inc(fin_done, 1)

            def head(h, first, adj_before, with_adj):
                dve.wait_ge(abc_loaded, 16 * h + 16)
                row = abc[:, bass.ds(h % 2, 1), :].rearrange("p o n -> p (o n)")
                for jt in range(NT):
                    slot = tring[:, jt % RING, :]
                    if jt in DVE_TILES:
                        dve.wait_ge(t_free, NT * h + jt + 1)
                        dve.scalar_tensor_tensor(out=slot, in0=row, scalar=ab[:, jt, bass.ds(h + H, 1)],
                                                 in1=adjT[:, jt, :], op0=ALU.is_gt, op1=ALU.mult).then_inc(t_ready, 1)
                    else:
                        n = sum(j not in DVE_TILES for j in range(jt + 1))
                        dve.wait_ge(u_ready, ACT_TILES * h + n)
                        dve.tensor_tensor(slot, adjT[:, jt, :], slot, ALU.is_gt).then_inc(t_ready, 1)
                    if jt % RING == ADJ_AT:
                        u = jt // RING
                        if adj_before if jt < RING else with_adj:
                            s = ADJ_EARLY + STEPS * h + u - 1
                            adj_sum(s, (u - 1) % 2, s % NT, s // NT)
                    if not first and FINISH_AT <= jt < FINISH_AT + 4:
                        finish_head(h, jt - FINISH_AT)

            dve.wait_ge(vp_ready, 2 + H)
            dve.wait_ge(r_out, 1)
            head(0, True, False, True)
            with dve.Fori(1, ADJ_HEADS) as h:
                head(h, False, True, True)
            head(ADJ_HEADS, False, True, False)
            with dve.Fori(ADJ_HEADS + 1, H) as h:
                head(h, False, False, False)
            for step in range(4):
                finish_head(H, step)

            dve.wait_ge(fin_done, 1 + H)
            dens = acc[:].rearrange("p t (h c) -> p t h c", c=HW)[:, :, :, DH]
            dve.reciprocal(rden, dens).then_inc(den_inv, 1)
            dve.wait_ge(den_inv, 1)
            dve.tensor_tensor(rden, rden, vsc[:].unsqueeze(1).to_broadcast([P, NT, H]), ALU.mult).then_inc(rden_ready, 1)
            dve.wait_ge(bout_loaded, 16)

            def tail(i, r):
                q = 1 - r
                if live(i, 0):
                    dve.wait_ge(z_made, i + 1)
                    dve.tensor_tensor(zt[:, r, :], bank[2 + r][:], bout, ALU.add).then_inc(z_ready, 1)
                if live(i, 1):
                    dve.wait_ge(e_ready, i)
                    if past(i, 3):
                        dve.wait_ge(out_ready, i - 2)
                    dve.scalar_tensor_tensor(out=yt[:, q, :], in0=zt[:, q, :], scalar=0.0, in1=et[:, q, :],
                                             op0=ALU.max, op1=ALU.add).then_inc(elu_ready, 1)
                if live(i, 0):
                    dve.wait_ge(z_ready, i + 1)
                    dve.tensor_scalar(et[:, r, :], zt[:, r, :], 0.0, None, ALU.min).then_inc(zmin_ready, 1)
                if live(i, 1):
                    dve.wait_ge(elu_ready, i)
                    dve.wait_ge(xr_loaded[q], 8 * (i + r))
                    dve.scalar_tensor_tensor(out=yt[:, q, :], in0=yt[:, q, :], scalar=-1.0, in1=xr[:, q, :],
                                             op0=ALU.add, op1=ALU.add).then_inc(y_ready, 1)
                if live(i, 2):
                    dve.wait_ge(rstd_ready, i - 1)
                    if past(i, 4):
                        dve.wait_ge(stored[r], 8 * (i - r - 2))
                    dve.tensor_scalar(ot[:, r, :], yt[:, r, :], mv[:, r, 0:1], rstd[:, r:r + 1],
                                      ALU.subtract, ALU.mult).then_inc(out_ready, 1)
                if live(i, 1):
                    dve.wait_ge(y_ready, i)
                    dve.bn_stats(stats[:, q, :], yt[:, q, :]).then_inc(stats_ready, 1)
                    dve.wait_ge(stats_ready, i)
                    dve.sem_inc(gate_dve, 1)
                    dve.bn_aggr(mv[:, q, :], stats[:, q, :]).then_inc(mv_ready, 1)

            over_tiles(dve, tail)

        @block.gpsimd
        def _(pool):
            pool.memset(idf[:], 0.0).then_inc(ident0, 1)
            pool.memset(idb, 0.0).then_inc(ident0, 1)
            pool.wait_ge(ident0, 2)
            for t in (idf[:], idb):
                pool.affine_select(out=t, in_=t, compare_op=ALU.not_equal, fill=1.0, base=0,
                                   pattern=[[-1, P]], channel_multiplier=1).then_inc(ident, 1)

            pool.wait_ge(w_loaded, 16)
            pool.wait_ge(a12_loaded, 32)
            pool.tensor_tensor(wtmp[1], W_sb.rearrange("p k (h d) -> p k h d", h=H),
                               a12[:, DH:2 * DH].unsqueeze(1).unsqueeze(1).to_broadcast([P, KT, H, DH]), ALU.mult).then_inc(wa_prod[1], 1)

            pool.wait_ge(e_scaled, 1)
            with pool.Fori(0, H // 2) as k:
                for r in range(2):
                    h = 2 * k + r
                    pool.wait_ge(xp_read, h + 1)
                    pool.sem_inc(gate, 1)
                    pool.tensor_tensor(xp[0][r], seq[:, :, bass.ds(h * DH, DH)],
                                       E[:, :, 0, bass.ds(h, 1)].to_broadcast([P, NT, DH]), ALU.mult).then_inc(xp_made[0], 1)

            pool.wait_ge(rden_ready, 1)
            pool.memset(mhalf, -0.5).then_inc(mhalf_set, 1)

            def hidden(i, slot):
                vals = acc[:, bass.ds(i, 1), :].rearrange("p t (h c) -> p (t h) c", c=HW)[:, :, 0:DH]
                inv = rden[:, bass.ds(i, 1), :].rearrange("p t h -> p (t h)").unsqueeze(2).to_broadcast([P, H, DH])
                if not isinstance(i, int):
                    pool.wait_ge(h_turned, i - HID + 1)
                    pool.sem_inc(gate, 1)
                pool.tensor_tensor(hid[:, slot, :].rearrange("p (h d) -> p h d", h=H), vals, inv, ALU.mult).then_inc(hid_ready, 1)

            def inverse_deviation(i, r):
                pool.wait_ge(mv_ready, i + 1)
                pool.sem_inc(gate, 1)
                pool.tensor_scalar(rstd[:, r:r + 1], mv[:, r, 1:2], EPS, None, ALU.add).then_inc(v_eps, 1)
                pool.wait_ge(v_eps, i + 1)
                pool.tensor_tensor(rstd[:, r:r + 1], rstd[:, r:r + 1], mhalf, ALU.pow).then_inc(rstd_ready, 1)

            for i in range(HID):
                hidden(i, i)
            pool.wait_ge(mhalf_set, 1)
            with pool.Fori(0, NT // HID - 1) as k:
                for q in range(HID):
                    inverse_deviation(HID * k + q, q % 2)
                    hidden(HID * k + q + HID, q)
            for i in range(NT - HID, NT):
                inverse_deviation(i, i % 2)


_INS = ["x", "adj", "L0_gnn_W_seq", "L0_gnn_a1", "L0_gnn_a2", "L0_gnn_W_out", "L0_gnn_b_out"]


def kernel(**inputs):
    import numpy as _np
    import concourse.bacc as _bacc
    from concourse import mybir as _mybir
    from concourse.bass_utils import run_bass_kernel_spmd as _run

    nc = _bacc.Bacc("TRN2", target_bir_lowering=False, num_devices=1)
    arrays, args = {}, []
    for name in _INS:
        a = _np.ascontiguousarray(inputs[name])
        arrays[f"in_{name}_dram"] = a
        args.append(nc.dram_tensor(f"in_{name}_dram", a.shape, _mybir.dt.from_np(a.dtype), kind="ExternalInput").ap())
    args.append(nc.dram_tensor("out_0_dram", (N, D), F32, kind="ExternalOutput").ap())
    gat_kernel(nc, *args)
    r = _run(nc, [arrays], core_ids=[0])
    return r.results[0]["out_0_dram"]
```

```python
from contextlib import ExitStack

import concourse.bass as bass
from concourse import mybir

F32 = mybir.dt.float32
F16 = mybir.dt.float16
BF16 = mybir.dt.bfloat16
U32 = mybir.dt.uint32
ALU = mybir.AluOpType
ACT = mybir.ActivationFunctionType
AX = mybir.AxisListType

P = 128
N, D, H, DH = 2048, 512, 16, 32
NT = N // P
KT = D // P
SLOPE = 0.2
EPS = 1e-5

HW = DH + 1
VW = 2 * HW
LO = 2.0 ** 11
TOP = 2.0 ** 13
SIGN_SCALE = 2.0 ** 60
TINY = 2.0 ** -100

RING = 4
EARLY_HEADS = 4
RING2 = RING + EARLY_HEADS
GRP = 4
GROUPS = H // GRP
ITB = 3
BANKS = -(-NT // ITB)
STEP = 4
STEPS = NT // STEP
ADJ_EARLY = 12
ADJ_HEADS = (GROUPS * NT - ADJ_EARLY) // STEPS
DVE_TILES = (3, 7, 11, 15)
DVE_LAST = (3, 7, 11)
ACT_TILES = NT - len(DVE_TILES)
SUMS_AT = 2
ADJ_AT = 0
ADJ_LAG = 2
FINISH_AT = (3, 7, 11, 14, 15)


def gat_kernel(nc, x, adj, W_seq, a1, a2, W_out, b_out, out):
    with ExitStack() as ctx:
        def sb(name, shape, dt):
            return ctx.enter_context(nc.sbuf_tensor(name, shape, dt))

        def sem(name):
            return ctx.enter_context(nc.semaphore(name))

        adjT = sb("adjT", [P, NT, N], BF16)
        Vp = sb("Vp", [P, H, NT, 2, VW], F16)
        acc = sb("acc", [P, NT, H * HW], F32)
        abc = sb("abc", [P, 2, N], F32)
        tring = sb("tring", [P, RING, N], BF16)
        wide = sb("wide", [P, 2 * NT * VW], F32)
        ab = sb("ab", [P, NT, 2 * H], F32)
        nbs = sb("nbs", [P, NT, H], F32)
        idf = sb("idf", [P, P], F32)
        vsc = sb("vsc", [P, H], F32)

        OFF = H * HW - D
        seq = acc[:, :, OFF:]
        xs = abc[:, 1, 0:2 * D].rearrange("p (r n) -> p r n", r=2)
        xT = abc[:, 1, 2 * D:4 * D].rearrange("p (r n) -> p r n", r=2)
        aT = abc[0:H, 0, :]
        E = abc[:, 1, 0:2 * NT * H].rearrange("p (t s h) -> p t s h", t=NT, s=2)
        elo = abc[:, 1, 2 * NT * H:4 * NT * H].rearrange("p (t c) -> p t c", t=NT)
        Es = abc[:, 1, 4 * NT * H:6 * NT * H].rearrange("p (t s h) -> p t s h", t=NT, s=2)
        misc = abc[:, 1, 6 * NT * H:N]
        mx, diag, ones, mcol = misc[:, 0:32], misc[:, 32:64], misc[:, 64:64 + P], misc[:, 200:201]
        Mb = misc[:, 208:208 + 2 * H]
        vinv = misc[:, 240:240 + 2 * H].rearrange("p (s h) -> p s h", s=2)
        tring32 = tring[:].rearrange("p r n -> p (r n)").bitcast(F32)
        tslot = [tring[:, r, :] for r in range(RING)]
        tslot += [Vp[:, e].rearrange("p t s c -> p (t s c)").bitcast(BF16)[:, 0:N] for e in range(EARLY_HEADS)]
        stage = tring32.rearrange("p (r n) -> p r n", r=2)
        xp = [[tring32[:, N + (2 * s + r) * NT * DH:N + (2 * s + r + 1) * NT * DH].rearrange("p (t d) -> p t d", t=NT)
               for r in range(2)] for s in range(2)]
        adjb = wide[:, 0:N].bitcast(BF16).rearrange("p (r n) -> p r n", r=2)
        raw = wide[:].rearrange("p (t s c) -> p t s c", s=2, c=VW)
        before = Vp[:].rearrange("p h t s c -> p (h t s c)")
        idb = before[:, 0:P].bitcast(BF16)
        half = D // 2
        WC = half + H
        Wx = before.bitcast(F32)[:, P:P + 2 * KT * WC].rearrange("p (k s c) -> p k s c", k=KT, s=2)
        deg, noedge = before[:, P:P + 4].bitcast(F32), before[:, P + 4:P + 8].bitcast(F32)

        Wo_sb = abc[:, 0, :].rearrange("p (k n) -> p k n", k=KT)
        free = Vp[:].rearrange("p h t s c -> p (h t s c)").bitcast(F32)

        def ring(k):
            return free[:, 2 * k * D:2 * (k + 1) * D].rearrange("p (r n) -> p r n", r=2)
        xr, hT, zt, et, yt, ot = (ring(k) for k in range(6))
        HID = 4
        hid = free[:, 18 * D:(18 + HID) * D].rearrange("p (r n) -> p r n", r=HID)
        bout = free[:, 14 * D:15 * D]
        rden = free[:, 15 * D:15 * D + NT * H].rearrange("p (t h) -> p t h", t=NT)
        stats = free[:, 16 * D:16 * D + 12].rearrange("p (r c) -> p r c", r=2)
        mv = free[:, 16 * D + 12:16 * D + 16].rearrange("p (r c) -> p r c", r=2)
        rstd = free[:, 16 * D + 16:16 * D + 18]
        mhalf = free[:, 16 * D + 18:16 * D + 19]
        a12 = adjT[:, 0, 0:4 * DH].bitcast(F32)
        wtmp = [acc[:, (2 + r) * KT:(3 + r) * KT, OFF:].rearrange("p k (h d) -> p k h d", h=H) for r in range(2)]

        bank = [ctx.enter_context(nc.psum_tensor(f"bank{k}", [P, 512], F32)) for k in range(8)]
        scratch = nc.dram_tensor("a_rows", [H, N], F32, kind="Internal")

        w_loaded, a12_loaded = [sem(f"w_loaded{k}") for k in range(KT)], sem("a12_loaded")
        x_loaded = [sem("x_loaded0"), sem("x_loaded1")]
        adj_loaded = [sem("adj_loaded0"), sem("adj_loaded1")]
        abc_loaded = sem("abc_loaded")
        wo_loaded, bout_loaded, a_stored = sem("wo_loaded"), sem("bout_loaded"), sem("a_stored")
        xr_loaded = [sem("xr_loaded0"), sem("xr_loaded1")]
        stored = [sem("stored0"), sem("stored1")]
        ident0, ident = sem("ident0"), sem("ident")
        wa_prod, wa_ready = [sem("wa_prod1"), sem("wa_prod2")], sem("wa_ready")
        x_turned, x_copied, seq_made, seq_copied = (sem(s) for s in ("x_turned", "x_copied", "seq_made", "seq_copied"))
        adj_cast, adj_fixed, adj_turned, adj_ready = (sem(s) for s in ("adj_cast", "adj_fixed", "adj_turned", "adj_ready"))
        noedge_set = sem("noedge_set")
        a_turned, a_copied = sem("a_turned"), sem("a_copied")
        dve_step = sem("dve_step")
        mx_turned, mx_spread = sem("mx_turned"), sem("mx_spread")
        e_in, e_out, r_in, r_out, e_scaled = (sem(s) for s in ("e_in", "e_out", "r_in", "r_out", "e_scaled"))
        ones_hi, vp_ready = sem("ones_hi"), sem("vp_ready")
        xp_made = [sem("xp_made_a"), sem("xp_made_b")]
        vp_hi = [sem("vp_hi_a"), sem("vp_hi_b")]
        xp_read, nbs_ready = sem("xp_read"), sem("nbs_ready")
        u_ready, t_ready, t_free = sem("u_ready"), sem("t_ready"), sem("t_free")
        bank_done, sums_copied, fin_done = (sem(s) for s in ("bank_done", "sums_copied", "fin_done"))
        adj_done, gsum_ready, part_sum = sem("adj_done"), sem("gsum_ready"), sem("part_sum")
        fin_sub, fin_mul = sem("fin_sub"), sem("fin_mul")
        rden_ready, hid_ready, h_turned, h_copied, z_made = (sem(s) for s in ("rden_ready", "hid_ready", "h_turned", "h_copied", "z_made"))
        z_ready, zmin_ready, e_ready, elu_ready, y_ready = (sem(s) for s in ("z_ready", "zmin_ready", "e_ready", "elu_ready", "y_ready"))
        stats_ready, mv_ready, v_eps, rstd_ready, out_ready = (sem(s) for s in ("stats_ready", "mv_ready", "v_eps", "rstd_ready", "out_ready"))
        gate, gate_dve, gate_sp = sem("gate"), sem("gate_dve"), sem("gate_sp")
        den_inv, mhalf_set = sem("den_inv"), sem("mhalf_set")

        block = ctx.enter_context(nc.Block())

        x_t = x.rearrange("(t p) d -> t p d", p=P)
        out_t = out.rearrange("(t p) d -> t p d", p=P)
        adj_t = adj.rearrange("(t p) n -> t p n", p=P)

        def live(i, lag):
            return not isinstance(i, int) or lag <= i < NT + lag

        def past(i, n):
            return not isinstance(i, int) or i >= n

        def over_tiles(eng, body, slots=2):
            for i in range(4):
                body(i, i % slots)
            with eng.Fori(4 // slots, NT // slots) as k:
                for q in range(slots):
                    body(slots * k + q, q)
            for i in (NT, NT + 1):
                body(i, i % slots)

        @block.sync
        def _(sp):
            sp.dma_start(xs[:, 0, :], x_t[0]).then_inc(x_loaded[0], 16)
            for k in range(KT):
                sp.dma_start(Wx[:, k, :, 0:half], W_seq[k * P:(k + 1) * P, :].rearrange("p (s c) -> p s c", s=2)).then_inc(w_loaded[k], 16)
                if k == 0:
                    sp.dma_start(a12[:, 0:DH], a1.rearrange("(o d) -> o d", o=1).partition_broadcast(P)).then_inc(a12_loaded, 16)
                    sp.dma_start(a12[:, DH:2 * DH], a2.rearrange("(o d) -> o d", o=1).partition_broadcast(P)).then_inc(a12_loaded, 16)
            sp.dma_start(xs[:, 1, :], x_t[1]).then_inc(x_loaded[1], 16)
            for r in range(2):
                sp.dma_start(stage[:, r, :], adj_t[r]).then_inc(adj_loaded[r], 16)
            with sp.Fori(1, NT // 2) as k:
                for r in range(2):
                    t = 2 * k + r
                    sp.wait_ge(x_turned, t + 1)
                    sp.dma_start(xs[:, r, :], x_t[t]).then_inc(x_loaded[r], 16)
                    sp.wait_ge(adj_cast, t + 1)
                    sp.dma_start(stage[:, r, :], adj_t[t]).then_inc(adj_loaded[r], 16)
            sp.wait_ge(a_copied, 4)
            sp.dma_start(scratch[:, :], aT).then_inc(a_stored, 16)
            sp.wait_ge(a_stored, 16)
            sp.dma_start(abc[:, 0, :], scratch[0:1, :].partition_broadcast(P)).then_inc(abc_loaded, 16)
            sp.wait_ge(abc_loaded, 16)
            sp.wait_ge(vp_ready, 2 + H)
            sp.dma_start(abc[:, 1, :], scratch[1:2, :].partition_broadcast(P)).then_inc(abc_loaded, 16)
            with sp.Fori(1, H // 2) as k:
                for r in range(2):
                    h = 2 * k + r
                    sp.wait_ge(abc_loaded, 16 * h)
                    sp.sem_inc(gate_sp, 1)
                    sp.wait_ge(t_ready, NT * h - NT)
                    sp.dma_start(abc[:, r, :], scratch[bass.ds(h, 1), :].partition_broadcast(P)).then_inc(abc_loaded, 16)
            sp.wait_ge(t_ready, NT * (H - 1))
            sp.dma_start(Wo_sb, W_out.rearrange("(k p) n -> p k n", p=P)).then_inc(wo_loaded, 16)
            sp.wait_ge(t_free, RING2 + NT * H)
            sp.dma_start(bout, b_out.rearrange("(o d) -> o d", o=1).partition_broadcast(P)).then_inc(bout_loaded, 16)

            def tail(i, r):
                if live(i, 0):
                    if past(i, 2):
                        sp.wait_ge(y_ready, i - 1)
                    sp.dma_start(xr[:, r, :], x_t[i]).then_inc(xr_loaded[r], 16)
                if live(i, 2):
                    sp.wait_ge(out_ready, i - 1)
                    sp.dma_start(out_t[i - 2], ot[:, r, :]).then_inc(stored[r], 16)

            over_tiles(sp, tail)
            for q in range(2):
                sp.wait_ge(stored[q], 16 * NT // 2)

        @block.tensor
        def _(pe):
            pe.sem_inc(x_turned, 2)
            pe.sem_inc(seq_made, 2)
            pe.sem_inc(adj_turned, 4)
            pe.sem_inc(t_free, RING)
            pe.wait_ge(ident, 2)

            def turn_x(t, r, n):
                pe.wait_ge(x_loaded[r], 16 * n)
                pe.wait_ge(x_copied, t + 1)
                for k in range(KT):
                    mm = pe.transpose(bank[r][:, k * P:(k + 1) * P], xs[:, r, k * P:(k + 1) * P], idf[:])
                mm.then_inc(x_turned, 1)

            def project(t, r):
                pe.wait_ge(x_copied, 2 + t + 1)
                pe.wait_ge(seq_copied, t + 1)
                for k in range(KT):
                    pe.wait_ge(wa_ready, 2 * k + 2)
                    for s in range(2):
                        mm = pe.matmul(bank[2 + 2 * s + r][:, 0:WC], xT[:, r, k * P:(k + 1) * P], Wx[:, k, s, :],
                                       start=(k == 0), stop=(k == KT - 1))
                mm.then_inc(seq_made, 1)

            def turn_adj(it, r):
                pe.wait_ge(adj_fixed, it + 1)
                for half in range(2):
                    pe.wait_ge(adj_ready, 2 * it + half + 1)
                    for q in range(8):
                        j = 8 * half + q
                        mm = pe.transpose(bank[6 + half][:].bitcast(BF16)[:, q * P:(q + 1) * P],
                                          adjb[:, r, j * P:(j + 1) * P], idb)
                    mm.then_inc(adj_turned, 1)

            turn_x(0, 0, 1)
            with pe.Fori(0, NT // 2 - 1) as k:
                for r in range(2):
                    turn_x(2 * k + r + 1, 1 - r, k + 1 + r)
                    project(2 * k + r, r)
                    turn_adj(2 * k + r, r)
            turn_x(NT - 1, 1, NT // 2)
            project(NT - 2, 0)
            turn_adj(NT - 2, 0)
            project(NT - 1, 1)
            turn_adj(NT - 1, 1)

            pe.wait_ge(seq_copied, 2 + NT)
            for t in range(NT):
                mm = pe.transpose(bank[t // 4][0:H, t % 4 * P:(t % 4 + 1) * P], ab[:, t, 0:H], idf[:])
                if t % 4 == 3:
                    mm.then_inc(a_turned, 1)
            pe.wait_ge(dve_step, 3)
            pe.transpose(bank[4][0:2 * H, 0:P], mx, idf[:]).then_inc(mx_turned, 1)
            pe.wait_ge(dve_step, 5)
            pe.matmul(bank[5][:, 0:2 * H], ones[0:2 * H, :], diag[0:2 * H, :], start=True, stop=True).then_inc(mx_spread, 1)
            pe.wait_ge(adj_ready, 2 + 2 * NT)
            pe.wait_ge(a_copied, 4)

            def adj_product(r, it, g, js):
                for j in js:
                    for s in range(2):
                        mm = pe.matmul(bank[6 + r][:, 0:GRP * HW], adjT[:, j, bass.ds(it * P, P)],
                                       Vp[:, bass.ds(GRP * g, GRP), j, s, HW:VW],
                                       start=(j == 0 and s == 0), stop=(j == NT - 1 and s == 1))
                if j == NT - 1:
                    mm.then_inc(adj_done, 1)

            pe.wait_ge(vp_ready, 2 + GRP)
            with pe.Fori(0, ADJ_EARLY // 2) as k:
                for r in range(2):
                    pe.wait_ge(gsum_ready, 2 * k + r + 1)
                    adj_product(r, 2 * k + r, 0, range(NT))
            pe.wait_ge(vp_ready, 2 + H)

            def head(h, first, with_adj, ring=RING2, grow=0):
                for jt in range(NT):
                    u = jt // STEP
                    pe.wait_ge(t_ready, NT * h + jt + 1)
                    for it in range(NT):
                        b, c = it // ITB, it % ITB
                        if jt == 0 and c == 0 and not first:
                            pe.wait_ge(sums_copied, BANKS * h - BANKS + b + 1)
                        mm = pe.matmul(bank[b][:, c * 2 * VW:(c + 1) * 2 * VW],
                                       tslot[jt % ring][:, it * P:(it + 1) * P], Vp[:, h, jt, :, :],
                                       start=(jt == 0 and c == 0), stop=(jt == NT - 1), skip_group_check=True)
                        if jt == NT - 1 and c == ITB - 1:
                            mm.then_inc(bank_done, 1)
                    mm.then_inc(t_free, 1 + (grow if jt == NT - 1 else 0))
                    if with_adj:
                        s = ADJ_EARLY + STEPS * h + u
                        if jt % STEP == 0:
                            pe.wait_ge(gsum_ready, s + 1)
                        q = jt % STEP
                        adj_product(u % 2, s % NT, s // NT, range(q * STEPS, (q + 1) * STEPS))

            head(0, True, True, RING)
            with pe.Fori(1, EARLY_HEADS - 1) as h:
                head(h, False, True, RING)
            head(EARLY_HEADS - 1, False, True, RING, grow=EARLY_HEADS)
            with pe.Fori(EARLY_HEADS, ADJ_HEADS) as h:
                head(h, False, True)
            with pe.Fori(ADJ_HEADS, H) as h:
                head(h, False, False)

            pe.wait_ge(sums_copied, BANKS * H)
            pe.wait_ge(wo_loaded, 16)

            def tail(i, slot):
                r = slot % 2
                if live(i, 0):
                    pe.wait_ge(hid_ready, i + 1)
                    if past(i, 2):
                        pe.wait_ge(h_copied, i - 1)
                    for k in range(KT):
                        mm = pe.transpose(bank[r][:, k * P:(k + 1) * P], hid[:, slot, k * P:(k + 1) * P], idf[:])
                    mm.then_inc(h_turned, 1)
                if live(i, 1):
                    q = 1 - r
                    pe.wait_ge(h_copied, i)
                    if past(i, 3):
                        pe.wait_ge(z_ready, i - 2)
                    for k in range(KT):
                        mm = pe.matmul(bank[2 + q][:], hT[:, q, k * P:(k + 1) * P], Wo_sb[:, k, :],
                                       start=(k == 0), stop=(k == KT - 1))
                    mm.then_inc(z_made, 1)

            over_tiles(pe, tail, HID)

        @block.scalar
        def _(act):
            act.sem_inc(x_copied, 2)
            act.sem_inc(adj_cast, 2)

            def copy_x(t, r):
                act.wait_ge(x_turned, 2 + t + 1)
                act.wait_ge(seq_made, t + 1)
                act.copy(xT[:, r, :], bank[r][:]).then_inc(x_copied, 1)

            def cast_adj(it, r, n):
                act.wait_ge(adj_loaded[r], 16 * n)
                act.wait_ge(adj_turned, 2 * it + 2)
                act.activation(adjb[:, r, :], stage[:, r, :], ACT.Copy, accum_out=deg[:, r:r + 1]).then_inc(adj_cast, 1)

            with act.Fori(0, NT // 2) as k:
                for r in range(2):
                    copy_x(2 * k + r, r)
                    cast_adj(2 * k + r, r, k + 1)

            for c in range(4):
                act.wait_ge(a_turned, c + 1)
                act.copy(aT[:, c * 512:(c + 1) * 512], bank[c][0:H, :]).then_inc(a_copied, 1)
            act.wait_ge(e_in, 1)
            act.activation(E[:, :, 1, :], E[:, :, 0, :], ACT.Exp, scale=-SLOPE).then_inc(e_out, 1)
            act.wait_ge(e_out, 1)
            act.activation(E[:, :, 0, :], E[:, :, 0, :], ACT.Exp, scale=-1.0).then_inc(e_out, 1)
            act.wait_ge(r_in, 1)
            act.activation(ab[:, :, 0:H], ab[:, :, 0:H], ACT.Exp, scale=SLOPE - 1.0).then_inc(r_out, 1)
            act.wait_ge(e_out, 2)
            act.activation(Vp[:, :, :, 0, DH], E[:, :, 0, :].rearrange("p t h -> p h t"), ACT.Copy, scale=TOP).then_inc(ones_hi, 1)
            act.activation(Vp[:, :, :, 0, HW + DH], E[:, :, 1, :].rearrange("p t h -> p h t"), ACT.Copy, scale=TOP).then_inc(ones_hi, 1)

            def copy_adj_sums(s, r, it, g):
                act.wait_ge(adj_done, s + 1)
                act.activation(acc[:, bass.ds(it, 1), bass.ds(GRP * HW * g, GRP * HW)].rearrange("p t c -> p (t c)"),
                               bank[6 + r][:, 0:GRP * HW], ACT.Copy).then_inc(gsum_ready, 1)

            def split_high(h, r):
                for s in range(2):
                    act.wait_ge(xp_made[s], h + 1)
                    act.activation(Vp[:, h, :, 0, s * HW:s * HW + DH], xp[s][r], ACT.Copy,
                                   scale=(1.0 / LO, 1.0)[s]).then_inc(vp_hi[s], 1)

            act.sem_inc(gsum_ready, 2)
            with act.Fori(0, (H - ADJ_EARLY + ADJ_LAG) // 2) as k:
                for r in range(2):
                    split_high(2 * k + r, r)
            with act.Fori(0, (ADJ_EARLY - ADJ_LAG) // 2) as k:
                for r in range(2):
                    split_high(H - ADJ_EARLY + ADJ_LAG + 2 * k + r, r)
                    copy_adj_sums(2 * k + r, r, 2 * k + r, 0)

            def copy_sums(h, ring=RING2):
                act.wait_ge(fin_done, h)
                for b in range(BANKS):
                    n = min(ITB, NT - b * ITB)
                    if n == ITB:
                        act.wait_ge(bank_done, (BANKS - 1) * (h - 1) + b + 1)
                    else:
                        act.wait_ge(t_free, ring + NT * h)
                    act.activation(raw[:, b * ITB:b * ITB + n, :, :].rearrange("p t s c -> p (t s c)"),
                                   bank[b][:, 0:n * 2 * VW], ACT.Copy).then_inc(sums_copied, 1)

            def head(h, first, adj_before, with_adj, ring=RING2, dve_tiles=DVE_TILES):
                act.wait_ge(abc_loaded, 16 * h + 16)
                row = abc[:, bass.ds(h % 2, 1), :].rearrange("p o n -> p (o n)")
                for jt in range(NT):
                    if first and jt == 2:
                        act.wait_ge(vp_ready, 2 + H)
                    if jt not in dve_tiles:
                        act.wait_ge(t_free, NT * h + jt + 1)
                        act.activation(tslot[jt % ring], row, ACT.Relu, bias=nbs[:, jt, bass.ds(h, 1)],
                                       scale=-SIGN_SCALE).then_inc(u_ready, 1)
                    if jt == SUMS_AT and not first:
                        copy_sums(h, ring)
                    if jt % STEP == ADJ_AT:
                        u = jt // STEP - ADJ_LAG
                        if adj_before if u < 0 else with_adj:
                            s = ADJ_EARLY + STEPS * h + u
                            copy_adj_sums(s, u % 2, s % NT, s // NT)

            head(0, True, True, True, RING)
            with act.Fori(1, EARLY_HEADS) as h:
                head(h, False, True, True, RING)
            with act.Fori(EARLY_HEADS, ADJ_HEADS) as h:
                head(h, False, True, True)
            head(ADJ_HEADS, False, True, False)
            with act.Fori(ADJ_HEADS + 1, H - 1) as h:
                head(h, False, False, False)
            head(H - 1, False, False, False, dve_tiles=DVE_LAST)
            copy_sums(H)

            def tail(i, r):
                if live(i, 0):
                    act.wait_ge(h_turned, i + 1)
                    if past(i, 2):
                        act.wait_ge(z_made, i - 1)
                    act.copy(hT[:, r, :], bank[r][:]).then_inc(h_copied, 1)
                if live(i, 1):
                    act.wait_ge(zmin_ready, i)
                    act.activation(et[:, 1 - r, :], et[:, 1 - r, :], ACT.Exp).then_inc(e_ready, 1)

            over_tiles(act, tail)

        @block.vector
        def _(dve):
            dve.sem_inc(seq_copied, 2)
            dve.sem_inc(adj_ready, 2)
            dve.sem_inc(vp_ready, 2)
            dve.sem_inc(xp_read, 2)
            dve.sem_inc(fin_done, 1)

            dve.wait_ge(a12_loaded, 32)
            for k in range(KT):
                dve.wait_ge(w_loaded[k], 16)
                dve.tensor_tensor(wtmp[0][:, k].rearrange("p (s h) d -> p s h d", s=2),
                                  Wx[:, k, :, 0:half].rearrange("p s (h d) -> p s h d", d=DH),
                                  a12[:, 0:DH].unsqueeze(1).unsqueeze(1).to_broadcast([P, 2, H // 2, DH]), ALU.mult).then_inc(wa_prod[0], 1)
                for r in range(2):
                    dve.wait_ge(wa_prod[r], k + 1)
                    dve.tensor_reduce(Wx[:, k, r, half:WC], wtmp[r][:, k], AX.X, ALU.add).then_inc(wa_ready, 1)
            def copy_seq(t, r):
                dve.wait_ge(seq_made, 2 + t + 1)
                for s in range(2):
                    made = bank[2 + 2 * s + r]
                    dve.tensor_copy(seq[:, t, s * half:(s + 1) * half], made[:, 0:half])
                    dve.tensor_reduce(nbs[:, t, s * H // 2:(s + 1) * H // 2], made[:, 0:half].rearrange("p (h d) -> p h d", d=DH),
                                      AX.X, ALU.max, apply_absolute_value=True)
                dve.tensor_copy(ab[:, t, 0:H], bank[2 + r][:, half:WC])
                dve.tensor_scalar(ab[:, t, H:2 * H], bank[4 + r][:, half:WC], -1.0, None, ALU.mult).then_inc(seq_copied, 1)

            def fix_adj(it, r):
                dve.wait_ge(adj_cast, 2 + it + 1)
                dve.tensor_scalar(noedge[:, r:r + 1], deg[:, r:r + 1], 0.0, None, ALU.is_equal).then_inc(noedge_set, 1)
                dve.wait_ge(noedge_set, it + 1)
                dve.tensor_scalar(adjb[:, r, :], adjb[:, r, :], noedge[:, r:r + 1], None, ALU.max).then_inc(adj_fixed, 1)

            def copy_adj(it):
                for half in range(2):
                    dve.wait_ge(adj_turned, 4 + 2 * it + half + 1)
                    dve.tensor_copy(adjT[:, 8 * half:8 * half + 8, bass.ds(it * P, P)],
                                    bank[6 + half][:].bitcast(BF16).rearrange("p (j i) -> p j i", j=8)).then_inc(adj_ready, 1)

            with dve.Fori(0, NT // 2) as k:
                for r in range(2):
                    fix_adj(2 * k + r, r)
                    copy_seq(2 * k + r, r)
                    copy_adj(2 * k + r)

            dve.wait_ge(seq_copied, 2 + NT)
            dve.memset(ones, 1.0).then_inc(dve_step, 1)
            dve.tensor_reduce(mx[:, 0:H], ab[:, :, H:2 * H].rearrange("p t h -> p h t"), AX.X, ALU.min,
                              negate=True).then_inc(dve_step, 1)
            dve.tensor_reduce(mx[:, H:2 * H], nbs[:].rearrange("p t h -> p h t"), AX.X, ALU.max).then_inc(dve_step, 1)
            dve.wait_ge(mx_turned, 1)
            dve.tensor_reduce(mcol[0:2 * H, :], bank[4][0:2 * H, 0:P], AX.X, ALU.max).then_inc(dve_step, 1)
            dve.wait_ge(dve_step, 4)
            dve.tensor_scalar(diag[0:2 * H, :], idf[0:2 * H, 0:2 * H], mcol[0:2 * H, :], None, ALU.mult).then_inc(dve_step, 1)
            dve.tensor_scalar(nbs[:], ab[:, :, H:2 * H], SIGN_SCALE, None, ALU.mult).then_inc(nbs_ready, 1)
            dve.wait_ge(mx_spread, 1)
            dve.tensor_copy(Mb, bank[5][:, 0:2 * H]).then_inc(dve_step, 1)
            dve.wait_ge(dve_step, 6)
            Mrow = Mb[:, 0:H].unsqueeze(1).to_broadcast([P, NT, H])
            dve.tensor_tensor(E[:, :, 0, :], ab[:, :, H:2 * H], Mrow, ALU.add).then_inc(e_in, 1)
            dve.wait_ge(a_turned, 4)
            dve.tensor_tensor(ab[:, :, 0:H], ab[:, :, 0:H], Mrow, ALU.add).then_inc(dve_step, 1)
            dve.wait_ge(dve_step, 7)
            dve.tensor_scalar(ab[:, :, 0:H], ab[:, :, 0:H], 0.0, None, ALU.max).then_inc(r_in, 1)
            dve.tensor_scalar(vsc[:], Mb[:, H:2 * H], TINY, None, ALU.max).then_inc(dve_step, 1)
            dve.wait_ge(dve_step, 8)
            dve.tensor_scalar(vsc[:].bitcast(U32), vsc[:].bitcast(U32), 0x7F800000, None, ALU.bitwise_and).then_inc(dve_step, 1)
            dve.wait_ge(dve_step, 9)
            dve.reciprocal(vinv[:, 1, :], vsc[:]).then_inc(dve_step, 1)
            dve.wait_ge(dve_step, 10)
            dve.tensor_scalar(vinv[:, 0, :], vinv[:, 1, :], TOP * LO, None, ALU.mult).then_inc(dve_step, 1)
            dve.tensor_scalar(vinv[:, 1, :], vinv[:, 1, :], TOP, None, ALU.mult).then_inc(dve_step, 1)
            dve.wait_ge(dve_step, 12)
            dve.wait_ge(e_out, 2)
            for s in range(2):
                dve.tensor_tensor(Es[:, :, s, :], E[:, :, s, :], vinv[:, s, :].unsqueeze(1).to_broadcast([P, NT, H]),
                                  ALU.mult).then_inc(e_scaled, 1)
            for s in range(2):
                dve.tensor_scalar(elo[:, :, s * H:(s + 1) * H], E[:, :, s, :], TOP * (LO, 1.0)[s], None,
                                  ALU.mult).then_inc(dve_step, 1)
            dve.wait_ge(ones_hi, 2)
            dve.wait_ge(dve_step, 14)
            for s in range(2):
                dve.scalar_tensor_tensor(out=Vp[:, :, :, 1, s * HW + DH], in0=Vp[:, :, :, 0, s * HW + DH],
                                         scalar=(-LO, -1.0)[s], in1=elo[:, :, s * H:(s + 1) * H].rearrange("p t h -> p h t"),
                                         op0=ALU.mult, op1=ALU.add).then_inc(dve_step, 1)

            dve.wait_ge(e_scaled, 2)
            with dve.Fori(0, H // 2) as k:
                for r in range(2):
                    h = 2 * k + r
                    dve.wait_ge(vp_ready, h + 1)
                    dve.tensor_tensor(xp[1][r], seq[:, :, bass.ds(h * DH, DH)],
                                      Es[:, :, 1, bass.ds(h, 1)].to_broadcast([P, NT, DH]), ALU.mult).then_inc(xp_made[1], 1)
                for r in range(2):
                    h = 2 * k + r
                    for s in range(2):
                        dve.wait_ge(vp_hi[s], h + 1)
                        dve.scalar_tensor_tensor(out=Vp[:, h, :, 1, s * HW:s * HW + DH],
                                                 in0=Vp[:, h, :, 0, s * HW:s * HW + DH], scalar=(-LO, -1.0)[s],
                                                 in1=xp[s][r], op0=ALU.mult, op1=ALU.add).then_inc((xp_read, vp_ready)[s], 1)

            def finish_head(h, step, adj_sums, tiles=slice(0, NT), part=0):
                sums = acc[:, tiles, bass.ds(HW * (h - 1), HW)]
                low = raw[:, tiles, 1, :]
                cA, cB = raw[:, tiles, 0, 0:HW], raw[:, tiles, 0, HW:VW]
                if step == 0:
                    dve.wait_ge(sums_copied, BANKS * (h - 1) + -(-tiles.stop // ITB))
                    dve.tensor_tensor(cB, cB, low[:, :, HW:VW], ALU.add).then_inc(part_sum, 1)
                if step == 1:
                    dve.scalar_tensor_tensor(out=cA, in0=low[:, :, 0:HW], scalar=1.0 / LO, in1=cA,
                                             op0=ALU.mult, op1=ALU.add).then_inc(part_sum, 1)
                if step == 2:
                    dve.wait_ge(part_sum, 2 * (h + part))
                    dve.wait_ge(gsum_ready, 2 + adj_sums)
                    dve.tensor_tensor(cB, sums, cB, ALU.subtract).then_inc(fin_sub, 1)
                if step == 3:
                    dve.wait_ge(fin_sub, h + part)
                    R = ab[:, tiles, bass.ds(h - 1, 1)].to_broadcast([P, tiles.stop - tiles.start, HW])
                    dve.tensor_tensor(cB, cB, R, ALU.mult).then_inc(fin_mul, 1)
                if step == 4:
                    dve.wait_ge(fin_mul, h + part)
                    dve.tensor_tensor(sums, cA, cB, ALU.add).then_inc(fin_done, 1)

            def head(h, first, adj_sums, ring=RING2, dve_tiles=DVE_TILES):
                dve.wait_ge(abc_loaded, 16 * h + 16)
                row = abc[:, bass.ds(h % 2, 1), :].rearrange("p o n -> p (o n)")
                for jt in range(NT):
                    slot = tslot[jt % ring]
                    if jt in dve_tiles:
                        dve.wait_ge(t_free, NT * h + jt + 1)
                        dve.scalar_tensor_tensor(out=slot, in0=row, scalar=ab[:, jt, bass.ds(h + H, 1)],
                                                 in1=adjT[:, jt, :], op0=ALU.is_gt, op1=ALU.mult).then_inc(t_ready, 1)
                    else:
                        n = sum(j not in dve_tiles for j in range(jt + 1))
                        dve.wait_ge(u_ready, ACT_TILES * h + n)
                        dve.tensor_tensor(slot, adjT[:, jt, :], slot, ALU.is_gt).then_inc(t_ready, 1)
                    for step in range(5):
                        if not first and jt == FINISH_AT[step]:
                            finish_head(h, step, adj_sums)

            dve.wait_ge(vp_ready, 2 + H)
            dve.wait_ge(r_out, 1)
            head(0, True, None, RING)
            with dve.Fori(1, EARLY_HEADS) as h:
                head(h, False, ADJ_EARLY + STEPS * h, RING)
            with dve.Fori(EARLY_HEADS, ADJ_HEADS) as h:
                head(h, False, ADJ_EARLY + STEPS * h)
            with dve.Fori(ADJ_HEADS, H - 1) as h:
                head(h, False, GROUPS * NT)
            head(H - 1, False, GROUPS * NT, dve_tiles=DVE_LAST)
            dve.wait_ge(t_free, RING2 + NT * H)
            for part, tiles in enumerate((slice(0, ITB), slice(ITB, NT))):
                for step in range(5):
                    finish_head(H, step, GROUPS * NT, tiles, part)
                dve.wait_ge(fin_done, 1 + H + part)
                dens = acc[:, tiles].rearrange("p t (h c) -> p t h c", c=HW)[:, :, :, DH]
                dve.reciprocal(rden[:, tiles], dens).then_inc(den_inv, 1)
                dve.wait_ge(den_inv, 1 + part)
                dve.tensor_tensor(rden[:, tiles], rden[:, tiles],
                                  vsc[:].unsqueeze(1).to_broadcast([P, tiles.stop - tiles.start, H]),
                                  ALU.mult).then_inc(rden_ready, 1)
            dve.wait_ge(bout_loaded, 16)

            def tail(i, r):
                q = 1 - r
                if live(i, 0):
                    dve.wait_ge(z_made, i + 1)
                    dve.tensor_tensor(zt[:, r, :], bank[2 + r][:], bout, ALU.add).then_inc(z_ready, 1)
                if live(i, 1):
                    dve.wait_ge(e_ready, i)
                    if past(i, 3):
                        dve.wait_ge(out_ready, i - 2)
                    dve.scalar_tensor_tensor(out=yt[:, q, :], in0=zt[:, q, :], scalar=0.0, in1=et[:, q, :],
                                             op0=ALU.max, op1=ALU.add).then_inc(elu_ready, 1)
                if live(i, 0):
                    dve.wait_ge(z_ready, i + 1)
                    dve.tensor_scalar(et[:, r, :], zt[:, r, :], 0.0, None, ALU.min).then_inc(zmin_ready, 1)
                if live(i, 1):
                    dve.wait_ge(elu_ready, i)
                    dve.wait_ge(xr_loaded[q], 8 * (i + r))
                    dve.scalar_tensor_tensor(out=yt[:, q, :], in0=yt[:, q, :], scalar=-1.0, in1=xr[:, q, :],
                                             op0=ALU.add, op1=ALU.add).then_inc(y_ready, 1)
                if live(i, 2):
                    dve.wait_ge(rstd_ready, i - 1)
                    if past(i, 4):
                        dve.wait_ge(stored[r], 8 * (i - r - 2))
                    dve.tensor_scalar(ot[:, r, :], yt[:, r, :], mv[:, r, 0:1], rstd[:, r:r + 1],
                                      ALU.subtract, ALU.mult).then_inc(out_ready, 1)
                if live(i, 1):
                    dve.wait_ge(y_ready, i)
                    dve.bn_stats(stats[:, q, :], yt[:, q, :]).then_inc(stats_ready, 1)
                    dve.wait_ge(stats_ready, i)
                    dve.sem_inc(gate_dve, 1)
                    dve.bn_aggr(mv[:, q, :], stats[:, q, :]).then_inc(mv_ready, 1)

            over_tiles(dve, tail)

        @block.gpsimd
        def _(pool):
            pool.memset(idf[:], 0.0).then_inc(ident0, 1)
            pool.memset(idb, 0.0).then_inc(ident0, 1)
            pool.wait_ge(ident0, 2)
            for t in (idf[:], idb):
                pool.affine_select(out=t, in_=t, compare_op=ALU.not_equal, fill=1.0, base=0,
                                   pattern=[[-1, P]], channel_multiplier=1).then_inc(ident, 1)

            pool.wait_ge(a12_loaded, 32)
            for k in range(KT):
                pool.wait_ge(w_loaded[k], 16)
                pool.tensor_tensor(wtmp[1][:, k].rearrange("p (s h) d -> p s h d", s=2),
                                   Wx[:, k, :, 0:half].rearrange("p s (h d) -> p s h d", d=DH),
                                   a12[:, DH:2 * DH].unsqueeze(1).unsqueeze(1).to_broadcast([P, 2, H // 2, DH]), ALU.mult).then_inc(wa_prod[1], 1)

            pool.wait_ge(e_scaled, 1)
            with pool.Fori(0, H // 2) as k:
                for r in range(2):
                    h = 2 * k + r
                    pool.wait_ge(xp_read, h + 1)
                    pool.sem_inc(gate, 1)
                    pool.tensor_tensor(xp[0][r], seq[:, :, bass.ds(h * DH, DH)],
                                       Es[:, :, 0, bass.ds(h, 1)].to_broadcast([P, NT, DH]), ALU.mult).then_inc(xp_made[0], 1)

            pool.wait_ge(rden_ready, 1)
            pool.memset(mhalf, -0.5).then_inc(mhalf_set, 1)

            def hidden(i, slot):
                vals = acc[:, bass.ds(i, 1), :].rearrange("p t (h c) -> p (t h) c", c=HW)[:, :, 0:DH]
                inv = rden[:, bass.ds(i, 1), :].rearrange("p t h -> p (t h)").unsqueeze(2).to_broadcast([P, H, DH])
                if not isinstance(i, int):
                    pool.wait_ge(h_turned, i - HID + 1)
                    pool.sem_inc(gate, 1)
                pool.tensor_tensor(hid[:, slot, :].rearrange("p (h d) -> p h d", h=H), vals, inv, ALU.mult).then_inc(hid_ready, 1)

            def inverse_deviation(i, r):
                pool.wait_ge(mv_ready, i + 1)
                pool.sem_inc(gate, 1)
                pool.tensor_scalar(rstd[:, r:r + 1], mv[:, r, 1:2], EPS, None, ALU.add).then_inc(v_eps, 1)
                pool.wait_ge(v_eps, i + 1)
                pool.tensor_tensor(rstd[:, r:r + 1], rstd[:, r:r + 1], mhalf, ALU.pow).then_inc(rstd_ready, 1)

            for i in range(HID):
                if i == ITB:
                    pool.wait_ge(rden_ready, 2)
                hidden(i, i)
            pool.wait_ge(mhalf_set, 1)
            with pool.Fori(0, NT // HID - 1) as k:
                for q in range(HID):
                    hidden(HID * k + q + HID, q)
                    inverse_deviation(HID * k + q, q % 2)
            for i in range(NT - HID, NT):
                inverse_deviation(i, i % 2)


_INS = ["x", "adj", "L0_gnn_W_seq", "L0_gnn_a1", "L0_gnn_a2", "L0_gnn_W_out", "L0_gnn_b_out"]


def kernel(**inputs):
    import numpy as _np
    import concourse.bacc as _bacc
    from concourse import mybir as _mybir
    from concourse.bass_utils import run_bass_kernel_spmd as _run

    nc = _bacc.Bacc("TRN2", target_bir_lowering=False, num_devices=1)
    arrays, args = {}, []
    for name in _INS:
        a = _np.ascontiguousarray(inputs[name])
        arrays[f"in_{name}_dram"] = a
        args.append(nc.dram_tensor(f"in_{name}_dram", a.shape, _mybir.dt.from_np(a.dtype), kind="ExternalInput").ap())
    args.append(nc.dram_tensor("out_0_dram", (N, D), F32, kind="ExternalOutput").ap())
    gat_kernel(nc, *args)
    r = _run(nc, [arrays], core_ids=[0])
    return r.results[0]["out_0_dram"]
```
